# Optimizing a Trainium2 kernel written in Bass

```python
import numpy as np
import jax
import jax.numpy as jnp

def _softmax(x, axis=-1):
    return jax.nn.softmax(x, axis=axis)
def _gelu(x):
    return jax.nn.gelu(x, approximate=True)
def _silu(x):
    return jax.nn.silu(x)
def _sigmoid(x):
    return jax.nn.sigmoid(x)
def _layernorm(x, axis=-1, eps=1e-5):
    m = jnp.mean(x, axis=axis, keepdims=True)
    v = jnp.var(x, axis=axis, keepdims=True)
    return (x - m) / jnp.sqrt(v + eps)
def _scatter_add(tgt, idx, src, axis=0):
    return tgt.at[idx].add(src)
def _segment_sum(src, seg, n):
    return jax.ops.segment_sum(src, seg, n)

kernel_name = 'mk_conv_seq_d2_conv_nchw256_6929dd'

def setup_inputs(seed: int = 0):
    np.random.seed(seed)
    _w = jnp.asarray
    def _rec_inputs():
        import jax
        import jax.numpy as jnp
        _gk = jax.random.key(seed)
        x = -0.0002928 + 1 * jax.random.normal(jax.random.fold_in(_gk, 1), (4, 256, 64, 64), jnp.float32)
        return x
    x = _rec_inputs()
    def _L0_conv_setup():
        import jax, jax.numpy as jnp
        import numpy as np
        B, C, H, W = (4, 256, 64, 64)
        C4 = C // 4

        def _conv1x1(x, w, b):
            return jnp.einsum('bchw,oc->bohw', x, w) + b[None, :, None, None]
        key = jax.random.key(seed)
        ks = jax.random.split(key, 10)
        s_in = 1.0 / np.sqrt(C)
        s_mid = 1.0 / np.sqrt(C4)
        return {'x': jax.random.normal(ks[0], (B, C, H, W), dtype=jnp.float32), 'Wq': jax.random.normal(ks[1], (C4, C), dtype=jnp.float32) * s_in, 'bq': jax.random.normal(ks[2], (C4,), dtype=jnp.float32) * s_in, 'Wk': jax.random.normal(ks[3], (C4, C), dtype=jnp.float32) * s_in, 'bk': jax.random.normal(ks[4], (C4,), dtype=jnp.float32) * s_in, 'Wv': jax.random.normal(ks[5], (C4, C), dtype=jnp.float32) * s_in, 'bv': jax.random.normal(ks[6], (C4,), dtype=jnp.float32) * s_in, 'Wo': jax.random.normal(ks[7], (C, C4), dtype=jnp.float32) * s_mid, 'bo': jax.random.normal(ks[8], (C,), dtype=jnp.float32) * s_mid, 'gamma': jnp.full((1,), 0.5, dtype=jnp.float32)}
    _L0_conv_all = _L0_conv_setup()
    _L0_conv_in = {k: v for k, v in _L0_conv_all.items() if k in ('Wq', 'bq', 'Wk', 'bk', 'Wv', 'bv', 'Wo', 'bo', 'gamma', )}
    del _L0_conv_all

    def _L1_conv_setup():
        import jax, jax.numpy as jnp
        import numpy as np
        B, C, H, W = (4, 256, 64, 64)
        D = C // 8
        key = jax.random.key(seed)
        ks = jax.random.split(key, 8)
        s = 0.02
        return {'x': jax.random.normal(ks[0], (B, C, H, W), dtype=jnp.float32), 'Wq': jax.random.normal(ks[1], (D, C), dtype=jnp.float32) * s, 'bq': jax.random.normal(ks[2], (D,), dtype=jnp.float32) * s, 'Wk': jax.random.normal(ks[3], (D, C), dtype=jnp.float32) * s, 'bk': jax.random.normal(ks[4], (D,), dtype=jnp.float32) * s, 'Wv': jax.random.normal(ks[5], (C, C), dtype=jnp.float32) * s, 'bv': jax.random.normal(ks[6], (C,), dtype=jnp.float32) * s, 'gamma': jax.random.normal(ks[7], (1,), dtype=jnp.float32)}
    _L1_conv_all = _L1_conv_setup()
    _L1_conv_in = {k: v for k, v in _L1_conv_all.items() if k in ('Wq', 'bq', 'Wk', 'bk', 'Wv', 'bv', 'gamma', )}
    del _L1_conv_all

    return {
        "x": x,
        "L0_conv_Wq": _L0_conv_in["Wq"],
        "L0_conv_bq": _L0_conv_in["bq"],
        "L0_conv_Wk": _L0_conv_in["Wk"],
        "L0_conv_bk": _L0_conv_in["bk"],
        "L0_conv_Wv": _L0_conv_in["Wv"],
        "L0_conv_bv": _L0_conv_in["bv"],
        "L0_conv_Wo": _L0_conv_in["Wo"],
        "L0_conv_bo": _L0_conv_in["bo"],
        "L0_conv_gamma": _L0_conv_in["gamma"],
        "L1_conv_Wq": _L1_conv_in["Wq"],
        "L1_conv_bq": _L1_conv_in["bq"],
        "L1_conv_Wk": _L1_conv_in["Wk"],
        "L1_conv_bk": _L1_conv_in["bk"],
        "L1_conv_Wv": _L1_conv_in["Wv"],
        "L1_conv_bv": _L1_conv_in["bv"],
        "L1_conv_gamma": _L1_conv_in["gamma"],
    }

def reference(x, L0_conv_Wq, L0_conv_bq, L0_conv_Wk, L0_conv_bk, L0_conv_Wv, L0_conv_bv, L0_conv_Wo, L0_conv_bo, L0_conv_gamma, L1_conv_Wq, L1_conv_bq, L1_conv_Wk, L1_conv_bk, L1_conv_Wv, L1_conv_bv, L1_conv_gamma):
    import jax
    import jax.numpy as jnp
    def _L0_conv_ref(x, Wq, bq, Wk, bk, Wv, bv, Wo, bo, gamma):
        import jax, jax.numpy as jnp
        import numpy as np
        B, C, H, W = (4, 256, 64, 64)
        C4 = C // 4

        def _conv1x1(x, w, b):
            return jnp.einsum('bchw,oc->bohw', x, w) + b[None, :, None, None]
        b, c, h, w = x.shape
        hw = h * w
        q = _conv1x1(x, Wq, bq).reshape(b, -1, hw)
        k = _conv1x1(x, Wk, bk).reshape(b, -1, hw)
        v = _conv1x1(x, Wv, bv).reshape(b, -1, hw)
        energy = jnp.einsum('bcn,bcm->bnm', q, k)
        att = jax.nn.softmax(energy.reshape(b, hw * hw), axis=-1).reshape(b, hw, hw)
        out = jnp.einsum('bcm,bmn->bcn', v, att).reshape(b, -1, h, w)
        out = _conv1x1(out, Wo, bo)
        return gamma[0] * out + x

    def _L1_conv_ref(x, Wq, bq, Wk, bk, Wv, bv, gamma):
        import jax, jax.numpy as jnp
        import numpy as np
        B, C, H, W = (4, 256, 64, 64)
        D = C // 8
        b, c, h, w = x.shape
        n = h * w
        xf = x.reshape(b, c, n)
        q = jnp.einsum('dc,bcn->bdn', Wq, xf) + bq[None, :, None]
        k = jnp.einsum('dc,bcn->bdn', Wk, xf) + bk[None, :, None]
        v = jnp.einsum('ec,bcn->ben', Wv, xf) + bv[None, :, None]
        energy = jnp.einsum('bdi,bdj->bij', q, k)
        attention = jax.nn.softmax(energy, axis=-1)
        out = jnp.einsum('bcj,bij->bci', v, attention)
        out = out.reshape(b, c, h, w)
        return gamma[0] * out + x

    def _gn(v, G=32, eps=1e-5):
        B_, C_, H_, W_ = v.shape
        g = v.reshape(B_, G, C_ // G, H_, W_)
        m = jnp.mean(g, axis=(2, 3, 4), keepdims=True)
        s = jnp.var(g, axis=(2, 3, 4), keepdims=True)
        return ((g - m) / jnp.sqrt(s + eps)).reshape(v.shape)

    def _ln_c(v, eps=1e-6):
        m = jnp.mean(v, axis=1, keepdims=True)
        s = jnp.var(v, axis=1, keepdims=True)
        return (v - m) / jnp.sqrt(s + eps)

    def _ln_t(v, eps=1e-5):
        m = jnp.mean(v, axis=-1, keepdims=True)
        s = jnp.var(v, axis=-1, keepdims=True)
        return (v - m) / jnp.sqrt(s + eps)

    def _to_tokens(v):
        B_, C_, H_, W_ = v.shape
        return v.reshape(B_, C_, H_ * W_).transpose(0, 2, 1)
    def _from_tokens(t, like):
        B_, C_, H_, W_ = like.shape
        return t.transpose(0, 2, 1).reshape(B_, C_, H_, W_)

    x = _L0_conv_ref(x, L0_conv_Wq, L0_conv_bq, L0_conv_Wk, L0_conv_bk, L0_conv_Wv, L0_conv_bv, L0_conv_Wo, L0_conv_bo, L0_conv_gamma)
    x = _L1_conv_ref(x, L1_conv_Wq, L1_conv_bq, L1_conv_Wk, L1_conv_bk, L1_conv_Wv, L1_conv_bv, L1_conv_gamma)
    return x


_drawn_inputs = setup_inputs


def setup_inputs(seed=0):
    import zlib

    import numpy as np

    out = dict(_drawn_inputs(seed))
    spreads = {}
    factors = {'L0_conv_Wq': 8.0,
     'L0_conv_bq': 8.0,
     'L0_conv_Wk': 8.0,
     'L0_conv_bk': 8.0,
     'L0_conv_Wv': 7.669,
     'L0_conv_bv': 8.0,
     'L0_conv_Wo': 8.0,
     'L1_conv_Wq': 8.0,
     'L1_conv_bq': 8.0,
     'L1_conv_Wk': 8.0,
     'L1_conv_bk': 64.0,
     'L1_conv_Wv': 8.0,
     'L1_conv_bv': 64.0}
    for name, (base, spread) in spreads.items():
        noise = np.random.default_rng([zlib.crc32(name.encode()), seed]).standard_normal(out[name].shape)
        drawn = base * np.exp(spread * noise) if base else spread * noise
        out[name] = jnp.asarray(drawn.astype(out[name].dtype))
    for name, factor in factors.items():
        out[name] = (out[name] * factor).astype(out[name].dtype)
    return out
```

```python
import concourse.bass as bass
from concourse import mybir
from contextlib import ExitStack

F32 = mybir.dt.float32
F32R = mybir.dt.float32r
ALU = mybir.AluOpType
ACT = mybir.ActivationFunctionType
AX = mybir.AxisListType

P = 128
BATCH, C, N = 4, 256, 4096
CT = C // P
D0, D1 = C // 4, C // 8
NT = N // P
BANK = 512
NC = N // BANK
TPC = BANK // P

WIDE = 2048
HALVES = N // WIDE
MTILES = NT * HALVES

E0W = 1024
E0CH = N // E0W
STEPS0 = E0CH * NT
PAIRS = NT // 2
STEPS1 = NC * PAIRS

K1 = 3 * D1
K1R = K1 + 2
SLOTS = 4
LAG = 2

BQ0, BK0, BQ1, BK1, BO0, BV1, G0, G1, NPC = 0, 1, 2, 3, 4, 6, 8, 9, 10


def build(nc, x, wqk0, wv0, wo0, bv0, wqk1, wv1, percol, ident_d, out):
    ctx = ExitStack()
    with ctx:
        def sb(name, shape, dt):
            return ctx.enter_context(nc.sbuf_tensor(name, shape, dt))

        def sem(name):
            return ctx.enter_context(nc.semaphore(name))

        xs = sb("xs", [P, CT, N], F32)
        qs = sb("qs", [P, N], F32R)
        ks = sb("ks", [P, N], F32R)
        vs = sb("vs", [P, NT * 2 * C], F32R)
        v0 = vs[:, 0:NT * 2 * D0].rearrange("p (t h c) -> p t h c", t=NT, h=2)
        k0lo = vs[0:D0, N:2 * N]
        v1 = vs[:, :].rearrange("p (t h c) -> p t h c", t=NT, h=2)
        att = sb("att", [P, N], F32)
        zacc = att[:, 0:2 * BANK]
        raw = att[:, 2 * BANK:4 * BANK].rearrange("p (h n) -> p h n", h=CT)
        prob = sb("prob", [P, SLOTS, E0W], F32)
        phi = sb("phi", [P, SLOTS, E0W], F32R)
        plo = sb("plo", [P, SLOTS, E0W], F32R)
        vtmp = prob[:, 0, 0:TPC * D0]

        wqk0s = sb("wqk0s", [P, CT, 2 * P], F32)
        wv0s = sb("wv0s", [P, CT, D0], F32)
        wo0s = sb("wo0s", [P, C], F32)
        bv0s = sb("bv0s", [P, TPC * D0], F32)
        wqk1s = sb("wqk1s", [P, CT, 2 * K1R], F32)
        wv1s = sb("wv1s", [P, CT, C], F32)
        pc = sb("pc", [P, NPC], F32)
        ident = sb("ident", [P, P], F32)
        gbo = sb("gbo", [P, CT], F32)
        gbv = sb("gbv", [P, CT], F32)
        ones = sb("ones", [P, 1], F32)
        zeros = sb("zeros", [P, 2 * BANK], F32)
        rmax = sb("rmax", [P, MTILES], F32)
        sums = sb("sums", [P, STEPS0], F32)
        gmax = sb("gmax", [P, 1], F32)
        gmax_all = sb("gmax_all", [P, 1], F32)
        neg_max = sb("neg_max", [P, 1], F32)
        psum0 = sb("psum0", [P, 1], F32)
        psum0_all = sb("psum0_all", [P, 1], F32)
        rsum0 = sb("rsum0", [P, 1], F32)
        gscale0 = sb("gscale0", [P, 1], F32)
        row_max = sb("row_max", [P, NT], F32)
        neg_rows = sb("neg_rows", [P, NT, 2], F32R)
        rz = sb("rz", [P, TPC], F32)
        rzg = sb("rzg", [P, TPC], F32)

        ps = ctx.enter_context(nc.psum_tensor("ps", [P, 8, BANK], F32))

        x_loaded = [sem(f"x_loaded{n}") for n in range(NC)]
        w_loaded = sem("w_loaded")
        consts_set = sem("consts_set")
        passed = sem("passed")
        out_stored = sem("out_stored")
        p0_q = sem("p0_q")
        p0_k = sem("p0_k")
        p0_v = sem("p0_v")
        p0_qhi = sem("p0_qhi")
        p0_khi = sem("p0_khi")
        p0_vt = sem("p0_vt")
        p0_vhi = sem("p0_vhi")
        p0_done = sem("p0_done")
        m_energy = sem("m_energy")
        m_free = sem("m_free")
        gmax_part = sem("gmax_part")
        gmax_full = sem("gmax_full")
        neg_set = sem("neg_set")
        x_biased = sem("x_biased")
        s0_energy = sem("s0_energy")
        s0_exp = sem("s0_exp")
        s0_hi = sem("s0_hi")
        s0_lo = sem("s0_lo")
        s0_av = sem("s0_av")
        s0_out = sem("s0_out")
        sum_part = sem("sum_part")
        sum_full = sem("sum_full")
        rsum_set = sem("rsum_set")
        scale_set = sem("scale_set")
        wo_done = sem("wo_done")
        x1_ready = sem("x1_ready")
        p1_q = sem("p1_q")
        p1_k = sem("p1_k")
        p1_v = sem("p1_v")
        p1_qhi = sem("p1_qhi")
        p1_khi = sem("p1_khi")
        p1_vhi = sem("p1_vhi")
        p1_qlo = sem("p1_qlo")
        p1_klo = sem("p1_klo")
        p1_vlo = sem("p1_vlo")
        rows_max = sem("rows_max")
        rows_hi = sem("rows_hi")
        rows_lo = sem("rows_lo")
        rows_t = sem("rows_t")
        rows_in = sem("rows_in")
        s1_energy = sem("s1_energy")
        s1_exp = sem("s1_exp")
        s1_lo = sem("s1_lo")
        s1_sum = sem("s1_sum")
        s1_av = sem("s1_av")
        s1_out = sem("s1_out")
        z_part = sem("z_part")
        z_recip = sem("z_recip")
        z_scale = sem("z_scale")
        z_rows = sem("z_rows")
        y_scaled = sem("y_scaled")
        y_ready = sem("y_ready")

        def cols(n, w=BANK):
            return bass.ds(n * w, w)

        def settled(engine):
            engine.sem_inc(passed, 1)

        block = ctx.enter_context(nc.Block())

        @block.sync
        def _(sp):
            sp.dma_start(xs[:, :, 0:BANK], x[0, :, :, 0:BANK]).then_inc(x_loaded[0], 16)
            for dst, src in ((wqk0s, wqk0), (wv0s, wv0), (wo0s, wo0), (bv0s, bv0), (wqk1s, wqk1),
                             (wv1s, wv1), (pc, percol), (ident, ident_d)):
                sp.dma_start(dst[:], src).then_inc(w_loaded, 16)
            for n in range(1, NC):
                sp.dma_start(xs[:, :, n * BANK:(n + 1) * BANK],
                             x[0, :, :, n * BANK:(n + 1) * BANK]).then_inc(x_loaded[n], 16)
            with sp.Fori(0, BATCH - 1) as b:
                for n in range(NC):
                    c = slice(n * BANK, (n + 1) * BANK)
                    sp.wait_ge(y_ready, b * NC + (n + 2))
                    sp.dma_start(out[bass.ds(b, 1), :, :, c], xs[:, :, c]).then_inc(out_stored, 16)
                    sp.wait_ge(out_stored, b * (16 * NC) + 16 * (n + 1))
                    sp.dma_start(xs[:, :, c], x[bass.ds(b + 1, 1), :, :, c]).then_inc(x_loaded[n], 16)
            for n in range(NC):
                c = slice(n * BANK, (n + 1) * BANK)
                sp.wait_ge(y_ready, (BATCH - 1) * NC + n + 2)
                sp.dma_start(out[BATCH - 1, :, :, c], xs[:, :, c]).then_inc(out_stored, 16)
            sp.wait_ge(out_stored, 16 * NC * BATCH)

        @block.tensor
        def _(pe):
            mm = nc.tensor.matmul

            def project(dst, w, n):
                for c in range(CT):
                    last = mm(dst, w(c), xs[:, c, n * BANK:(n + 1) * BANK], start=c == 0, stop=c == CT - 1)
                return last

            def values(dst, w, n):
                for t in range(TPC):
                    for c in range(CT):
                        m = (n * TPC + t) * P
                        last = mm(dst(t), xs[:, c, m:m + P], w[:, c, :], start=c == 0, stop=c == CT - 1)
                return last

            def energy0(dst, t, n0):
                banks = dst.shape[1]
                for k in range(banks):
                    mm(dst[:, k, :], qs[:, t * P:(t + 1) * P], ks[:, bass.ds(n0 + k * BANK, BANK)],
                       start=True, stop=False)
                for k in range(banks):
                    last = mm(dst[:, k, :], qs[0:D0, t * P:(t + 1) * P],
                              k0lo[:, bass.ds(n0 + k * BANK, BANK)], start=False, stop=True)
                return last

            pe.wait_ge(w_loaded, 16 * 8)
            pe.sem_inc(s0_av, SLOTS)
            pe.sem_inc(s1_av, SLOTS)
            pe.sem_inc(z_part, 1)

            with pe.Fori(0, BATCH) as b:
                pe.wait_ge(y_ready, b * NC + 1)
                for n in range(NC):
                    pe.wait_ge(x_loaded[n], b * 16 + 16)
                    if n >= 2:
                        pe.wait_ge(p0_done, b * NC + (n - 1))
                    s = n % 2
                    project(ps[:, s, :], lambda c: wqk0s[:, c, 0:P], n).then_inc(p0_q, 1)
                    project(ps[:, 2 + s, :], lambda c: wqk0s[:, c, P:2 * P], n).then_inc(p0_k, 1)
                    values(lambda t: ps[:, 4 + s, t * D0:(t + 1) * D0], wv0s, n).then_inc(p0_v, 1)

                pe.wait_ge(p0_done, b * NC + NC)
                settled(pe)
                with pe.Fori(0, HALVES) as h:
                    for t in range(NT):
                        pe.wait_ge(m_free, b * (2 * MTILES) + h * NT + (t + 1))
                        s = 4 * (t % 2)
                        energy0(ps[:, s:s + 4, :], t, h * WIDE).then_inc(m_energy, 1)

                pe.wait_ge(m_free, b * (2 * MTILES) + (MTILES + 2))
                settled(pe)
                with pe.Fori(0, E0CH) as h:
                    def attend0(t):
                        pe.wait_ge(s0_lo, b * STEPS0 + h * NT + (t + 1 + SLOTS))
                        if t == 0:
                            pe.wait_ge(s0_out, b * E0CH + (h + 1))
                        for part in (phi, plo):
                            for k in range(E0W // BANK):
                                last = mm(ps[:, 6 + k, :], v0[:, t, :, :].rearrange("p h c -> p (h c)"),
                                          part[:, t % SLOTS, k * BANK:(k + 1) * BANK],
                                          start=t == 0 and part is phi, stop=t == NT - 1 and part is plo)
                        last.then_inc(s0_av, 1)

                    for t in range(NT):
                        pe.wait_ge(s0_exp, b * STEPS0 + h * NT + (t + (2 if t < 2 else 1)))
                        s = 2 * (t % 3)
                        energy0(ps[:, s:s + 2, :], t, h * E0W).then_inc(s0_energy, 1)
                        if t >= LAG:
                            attend0(t - LAG)
                    for t in range(NT - LAG, NT):
                        attend0(t)

                pe.wait_ge(s0_out, b * E0CH + (E0CH + 1))
                for n in range(NC):
                    c = slice(n * BANK, (n + 1) * BANK)
                    if n >= 2:
                        pe.wait_ge(x1_ready, b * NC + (n - 1))
                    for k in range(CT):
                        last = mm(ps[:, 2 * (n % 2) + k, :], wo0s[:, k * P:(k + 1) * P], att[:, c],
                                  start=True, stop=True)
                    last.then_inc(wo_done, 1)
                    pe.wait_ge(x1_ready, b * NC + (n + 1))
                    if n >= 1:
                        pe.wait_ge(p1_qlo, b * NC + n)
                    project(ps[0:K1, 4, :], lambda c: wqk1s[:, c, 0:K1], n).then_inc(p1_q, 1)
                    if n >= 1:
                        pe.wait_ge(p1_klo, b * NC + n)
                    project(ps[0:K1R, 5, :], lambda c: wqk1s[:, c, K1R:2 * K1R], n).then_inc(p1_k, 1)
                    if n >= 1:
                        pe.wait_ge(p1_vlo, b * NC + n)
                    values(lambda t: ps[:, 6 + t // 2, (t % 2) * C:(t % 2 + 1) * C], wv1s, n).then_inc(p1_v, 1)

                pe.wait_ge(p1_qlo, b * NC + NC)
                pe.wait_ge(p1_klo, b * NC + NC)
                pe.wait_ge(p1_vlo, b * NC + NC)
                settled(pe)
                with pe.Fori(0, HALVES) as h:
                    for t in range(NT):
                        pe.wait_ge(m_free, b * (2 * MTILES) + h * NT + (MTILES + t + 1))
                        for k in range(4):
                            last = mm(ps[:, 4 * (t % 2) + k, :], qs[0:K1, t * P:(t + 1) * P],
                                      ks[0:K1, bass.ds(h * WIDE + k * BANK, BANK)], start=True, stop=True)
                        last.then_inc(m_energy, 1)

                pe.wait_ge(rows_lo, b + 1)
                for t in range(NT):
                    last = mm(ps[0:2, t // TPC, (t % TPC) * P:(t % TPC + 1) * P],
                              neg_rows[:, t, :].bitcast(F32), ident[:], start=True, stop=True)
                last.then_inc(rows_t, 1)

                pe.wait_ge(rows_in, b * 2 + 2)
                settled(pe)
                with pe.Fori(0, NC) as n:
                    def attend1(u):
                        pe.wait_ge(s1_exp, b * (2 * STEPS1) + n * (2 * PAIRS) + (2 * u + 2 + 4))
                        if u == 0:
                            pe.wait_ge(s1_out, b * NC + (n + 1))
                        for part, lo in ((phi, 0), (phi, 1), (plo, 0)):
                            if part is plo:
                                pe.wait_ge(s1_lo, b * STEPS1 + n * PAIRS + (u + 1 + SLOTS))
                            for j in range(2):
                                for k in range(CT):
                                    last = mm(ps[:, 4 + k, :], v1[:, 2 * u + j, lo, k * P:(k + 1) * P],
                                              part[:, u % SLOTS, j * BANK:(j + 1) * BANK],
                                              start=u == 0 and j == 0 and part is phi and lo == 0,
                                              stop=u == PAIRS - 1 and j == 1 and part is plo)
                        last.then_inc(s1_av, 1)

                    for u in range(PAIRS):
                        pe.wait_ge(s1_exp, b * (2 * STEPS1) + n * (2 * PAIRS) + (2 * u + 2))
                        for j in range(2):
                            t = 2 * u + j
                            last = mm(ps[:, 2 * (u % 2) + j, :], ks[0:K1R, t * P:(t + 1) * P],
                                      qs[0:K1R, cols(n)], start=True, stop=True)
                        last.then_inc(s1_energy, 1)
                        if u >= 1:
                            attend1(u - 1)
                    attend1(PAIRS - 1)
                    pe.wait_ge(s1_sum, b * STEPS1 + n * PAIRS + (PAIRS + SLOTS))
                    for q in range(TPC):
                        for j in range(2):
                            last = mm(ps[:, 6, q:q + 1], zacc[:, j * BANK + q * P:j * BANK + (q + 1) * P],
                                      ones[:], start=j == 0, stop=j == 1)
                    last.then_inc(z_part, 1)
                    pe.wait_ge(z_scale, b * NC + (n + 1))
                    for q in range(TPC):
                        last = mm(ps[:, 7, q * P:(q + 1) * P], rzg[:, q:q + 1].to_broadcast([P, P]), ident[:],
                                  start=True, stop=True)
                    last.then_inc(z_rows, 1)

        @block.scalar
        def _(act):
            act.sem_inc(s0_exp, 3)
            act.sem_inc(s1_exp, 4)
            act.wait_ge(w_loaded, 16 * 8)
            with act.Fori(0, BATCH) as b:
                for n in range(NC):
                    c = slice(n * BANK, (n + 1) * BANK)
                    s = n % 2
                    act.wait_ge(p0_q, b * NC + (n + 1))
                    nc.scalar.activation(qs[:, c], ps[:, s, :], ACT.Identity,
                                         bias=pc[:, BQ0:BQ0 + 1]).then_inc(p0_qhi, 1)
                    act.wait_ge(p0_k, b * NC + (n + 1))
                    nc.scalar.activation(ks[:, c], ps[:, 2 + s, :], ACT.Identity,
                                         bias=pc[:, BK0:BK0 + 1]).then_inc(p0_khi, 1)
                    act.wait_ge(p0_vt, b * NC + (n + 1))
                    nc.scalar.copy(v0[:, n * TPC:(n + 1) * TPC, 0, :],
                                   vtmp.rearrange("p (t c) -> p t c", t=TPC)).then_inc(p0_vhi, 1)
                act.wait_ge(p0_done, b * NC + NC)
                act.wait_ge(consts_set, 3)
                for k in range(CT):
                    nc.scalar.activation(xs[:, k, :], xs[:, k, :], ACT.Identity,
                                         bias=gbo[:, k:k + 1]).then_inc(x_biased, 1)
                act.wait_ge(gmax_full, b + 1)
                nc.scalar.mul(neg_max[:], gmax_all[:], -1.0).then_inc(neg_set, 1)
                act.wait_ge(neg_set, b + 1)

                with act.Fori(0, E0CH) as h:
                    for t in range(NT):
                        act.wait_ge(s0_energy, b * STEPS0 + h * NT + (t + 1))
                        act.wait_ge(s0_lo, b * STEPS0 + h * NT + (t + 1))
                        s = 2 * (t % 3)
                        nc.scalar.activation(prob[:, t % SLOTS, :].rearrange("p (k n) -> p k n", k=2),
                                             ps[:, s:s + 2, :], ACT.Exp, bias=neg_max[:],
                                             accum_out=sums[:, bass.ds(h * NT + t, 1)]).then_inc(s0_exp, 1)

                for n in range(NC):
                    c = slice(n * BANK, (n + 1) * BANK)
                    act.wait_ge(p1_q, b * NC + (n + 1))
                    nc.scalar.activation(qs[0:K1, c], ps[0:K1, 4, :], ACT.Identity,
                                         bias=pc[0:K1, BQ1:BQ1 + 1]).then_inc(p1_qhi, 1)
                    act.wait_ge(p1_k, b * NC + (n + 1))
                    nc.scalar.activation(ks[0:K1R, c], ps[0:K1R, 5, :], ACT.Identity,
                                         bias=pc[0:K1R, BK1:BK1 + 1]).then_inc(p1_khi, 1)
                    act.wait_ge(p1_v, b * NC + (n + 1))
                    nc.scalar.copy(v1[:, n * TPC:(n + 1) * TPC, 0, :],
                                   ps[:, 6:8, :].rearrange("p k (t c) -> p (k t) c", c=C)).then_inc(p1_vhi, 1)
                act.wait_ge(rows_t, b + 1)
                for h in range(2):
                    nc.scalar.copy(qs[K1:K1R, h * WIDE:(h + 1) * WIDE].rearrange("p (k n) -> p k n", k=4),
                                   ps[0:2, 4 * h:4 * h + 4, :]).then_inc(rows_in, 1)

                with act.Fori(0, NC) as n:
                    for u in range(PAIRS):
                        act.wait_ge(s1_energy, b * STEPS1 + n * PAIRS + (u + 1))
                        act.wait_ge(s1_lo, b * STEPS1 + n * PAIRS + (u + 1))
                        act.wait_ge(s1_sum, b * STEPS1 + n * PAIRS + (u + 1))
                        s = 2 * (u % 2)
                        nc.scalar.activation(prob[:, u % SLOTS, :].rearrange("p (k n) -> p k n", k=2),
                                             ps[:, s:s + 2, :], ACT.Exp).then_inc(s1_exp, 1)
                        act.wait_ge(s1_av, b * STEPS1 + n * PAIRS + (u + 1))
                        nc.scalar.activation(phi[:, u % SLOTS, :].rearrange("p (k n) -> p k n", k=2),
                                             ps[:, s:s + 2, :], ACT.Exp).then_inc(s1_exp, 1)

        @block.gpsimd
        def _(pool):
            pool.wait_ge(consts_set, 1)
            pool.sem_inc(s1_sum, SLOTS)
            with pool.Fori(0, BATCH) as b:
                pool.wait_ge(gmax_part, b + 1)
                settled(pool)
                nc.gpsimd.partition_all_reduce(gmax_all[:], gmax[:], P,
                                               bass.bass_isa.ReduceOp.max).then_inc(gmax_full, 1)
                with pool.Fori(0, E0CH) as h:
                    for t in range(NT):
                        pool.wait_ge(s0_exp, b * STEPS0 + h * NT + (t + 1 + 3))
                        pool.wait_ge(s0_av, b * STEPS0 + h * NT + (t + 1))
                        settled(pool)
                        nc.gpsimd.tensor_scalar(phi[:, t % SLOTS, :], prob[:, t % SLOTS, :], 1.0, 0.0,
                                                ALU.mult, ALU.add).then_inc(s0_hi, 1)
                pool.wait_ge(sum_part, b + 1)
                settled(pool)
                nc.gpsimd.partition_all_reduce(psum0_all[:], psum0[:], P,
                                               bass.bass_isa.ReduceOp.add).then_inc(sum_full, 1)
                with pool.Fori(0, NC) as n:
                    pool.wait_ge(z_part, b * NC + (n + 1))
                    for u in range(PAIRS):
                        pool.wait_ge(s1_exp, b * (2 * STEPS1) + n * (2 * PAIRS) + (2 * u + 1 + 4))
                        if u >= 1:
                            pool.wait_ge(s1_sum, b * STEPS1 + n * PAIRS + (u + SLOTS))
                        nc.gpsimd.tensor_tensor(zacc, zacc if u else zeros[:], prob[:, u % SLOTS, :],
                                                ALU.add).then_inc(s1_sum, 1)

        @block.vector
        def _(dve):
            nc.vector.memset(zeros[:], 0.0).then_inc(consts_set, 1)
            nc.vector.memset(ones[:], 1.0)
            dve.sem_inc(m_free, 2)
            dve.sem_inc(s0_lo, SLOTS)
            dve.sem_inc(s1_lo, SLOTS)
            dve.sem_inc(s0_out, 1)
            dve.sem_inc(s1_out, 1)
            dve.sem_inc(y_ready, 1)
            dve.wait_ge(w_loaded, 16 * 8)
            nc.vector.tensor_scalar(gbo[:], pc[:, BO0:BO0 + CT], pc[:, G0:G0 + 1], None,
                                    ALU.mult).then_inc(consts_set, 1)
            nc.vector.tensor_scalar(gbv[:], pc[:, BV1:BV1 + CT], pc[:, G1:G1 + 1], None,
                                    ALU.mult).then_inc(consts_set, 1)
            with dve.Fori(0, BATCH) as b:
                def low(out, src, bias, hi):
                    return nc.vector.scalar_tensor_tensor(out=out, in0=src, scalar=bias, in1=hi.bitcast(F32),
                                                          op0=ALU.add, op1=ALU.subtract)

                for n in range(NC):
                    c = slice(n * BANK, (n + 1) * BANK)
                    s = n % 2
                    dve.wait_ge(p0_qhi, b * NC + (n + 1))
                    low(qs[D0:P, c], ps[D0:P, s, :], pc[D0:P, BQ0:BQ0 + 1], qs[D0:P, c])
                    dve.wait_ge(p0_khi, b * NC + (n + 1))
                    low(k0lo[:, c], ps[0:D0, 2 + s, :], pc[0:D0, BK0:BK0 + 1], ks[0:D0, c])
                    dve.wait_ge(p0_v, b * NC + (n + 1))
                    if n >= 1:
                        dve.wait_ge(p0_done, b * NC + n)
                    nc.vector.tensor_tensor(vtmp, ps[:, 4 + s, 0:TPC * D0], bv0s[:], ALU.add).then_inc(p0_vt, 1)
                    dve.wait_ge(p0_vhi, b * NC + (n + 1))
                    nc.vector.tensor_tensor(v0[:, n * TPC:(n + 1) * TPC, 1, :],
                                            vtmp.rearrange("p (t c) -> p t c", t=TPC),
                                            v0[:, n * TPC:(n + 1) * TPC, 0, :].bitcast(F32),
                                            ALU.subtract).then_inc(p0_done, 1)

                with dve.Fori(0, HALVES) as h:
                    for t in range(NT):
                        dve.wait_ge(m_energy, b * (2 * MTILES) + h * NT + (t + 1))
                        s = 4 * (t % 2)
                        nc.vector.tensor_reduce(rmax[:, bass.ds(h * NT + t, 1)], ps[:, s:s + 4, :], AX.XY,
                                                ALU.max).then_inc(m_free, 1)
                dve.wait_ge(m_free, b * (2 * MTILES) + (MTILES + 2))
                nc.vector.tensor_reduce(gmax[:], rmax[:], AX.X, ALU.max).then_inc(gmax_part, 1)

                with dve.Fori(0, E0CH) as h:
                    for t in range(NT):
                        dve.wait_ge(s0_hi, b * STEPS0 + h * NT + (t + 1))
                        nc.vector.tensor_tensor(plo[:, t % SLOTS, :], prob[:, t % SLOTS, :],
                                                phi[:, t % SLOTS, :].bitcast(F32),
                                                ALU.subtract).then_inc(s0_lo, 1)
                    dve.wait_ge(s0_av, b * STEPS0 + h * NT + (NT + SLOTS))
                    nc.vector.tensor_copy(att[:, bass.ds(h * E0W, E0W)].rearrange("p (k n) -> p k n", k=2),
                                          ps[:, 6:8, :]).then_inc(s0_out, 1)
                dve.wait_ge(s0_exp, b * STEPS0 + (STEPS0 + 3))
                nc.vector.tensor_reduce(psum0[:], sums[:], AX.X, ALU.add).then_inc(sum_part, 1)
                dve.wait_ge(sum_full, b + 1)
                nc.vector.reciprocal(rsum0[:], psum0_all[:]).then_inc(rsum_set, 1)
                dve.wait_ge(rsum_set, b + 1)
                nc.vector.tensor_scalar(gscale0[:], rsum0[:], pc[:, G0:G0 + 1], None,
                                        ALU.mult).then_inc(scale_set, 1)
                dve.wait_ge(scale_set, b + 1)
                dve.wait_ge(x_biased, b * CT + CT)

                for n in range(NC):
                    c = slice(n * BANK, (n + 1) * BANK)
                    dve.wait_ge(wo_done, b * NC + (n + 1))
                    s = 2 * (n % 2)
                    nc.vector.scalar_tensor_tensor(out=xs[:, :, c], in0=ps[:, s:s + 2, :], scalar=gscale0[:],
                                                   in1=xs[:, :, c], op0=ALU.mult, op1=ALU.add).then_inc(x1_ready, 1)
                    dve.wait_ge(p1_qhi, b * NC + (n + 1))
                    low(qs[D1:2 * D1, c], ps[D1:2 * D1, 4, :], pc[D1:2 * D1, BQ1:BQ1 + 1],
                        qs[D1:2 * D1, c]).then_inc(p1_qlo, 1)
                    dve.wait_ge(p1_khi, b * NC + (n + 1))
                    low(ks[2 * D1:K1, c], ps[2 * D1:K1, 5, :], pc[2 * D1:K1, BK1:BK1 + 1],
                        ks[2 * D1:K1, c]).then_inc(p1_klo, 1)
                    dve.wait_ge(p1_vhi, b * NC + (n + 1))
                    nc.vector.tensor_tensor(v1[:, n * TPC:(n + 1) * TPC, 1, :],
                                            ps[:, 6:8, :].rearrange("p k (t c) -> p (k t) c", c=C),
                                            v1[:, n * TPC:(n + 1) * TPC, 0, :].bitcast(F32),
                                            ALU.subtract).then_inc(p1_vlo, 1)

                with dve.Fori(0, HALVES) as h:
                    for t in range(NT):
                        dve.wait_ge(m_energy, b * (2 * MTILES) + h * NT + (MTILES + t + 1))
                        s = 4 * (t % 2)
                        nc.vector.tensor_reduce(rmax[:, bass.ds(h * NT + t, 1)], ps[:, s:s + 4, :], AX.XY,
                                                ALU.max).then_inc(m_free, 1)
                dve.wait_ge(m_free, b * (2 * MTILES) + (2 * MTILES + 2))
                nc.vector.tensor_tensor(row_max[:], rmax[:, 0:NT], rmax[:, NT:2 * NT], ALU.max).then_inc(rows_max, 1)
                dve.wait_ge(rows_max, b + 1)
                nc.vector.tensor_scalar(neg_rows[:, :, 0], row_max[:], -1.0, None, ALU.mult).then_inc(rows_hi, 1)
                dve.wait_ge(rows_hi, b + 1)
                nc.vector.scalar_tensor_tensor(out=neg_rows[:, :, 1], in0=row_max[:], scalar=-1.0,
                                               in1=neg_rows[:, :, 0].bitcast(F32), op0=ALU.mult,
                                               op1=ALU.subtract).then_inc(rows_lo, 1)

                with dve.Fori(0, NC) as n:
                    for u in range(PAIRS):
                        dve.wait_ge(s1_exp, b * (2 * STEPS1) + n * (2 * PAIRS) + (2 * u + 2 + 4))
                        nc.vector.tensor_tensor(plo[:, u % SLOTS, :], prob[:, u % SLOTS, :],
                                                phi[:, u % SLOTS, :].bitcast(F32),
                                                ALU.subtract).then_inc(s1_lo, 1)
                    dve.wait_ge(s1_av, b * STEPS1 + n * PAIRS + (PAIRS + SLOTS))
                    nc.vector.tensor_copy(raw, ps[:, 4:6, :]).then_inc(s1_out, 1)
                    dve.wait_ge(z_part, b * NC + (n + 2))
                    nc.vector.reciprocal(rz[:], ps[:, 6, 0:TPC]).then_inc(z_recip, 1)
                    dve.wait_ge(z_recip, b * NC + (n + 1))
                    nc.vector.tensor_scalar(rzg[:], rz[:], pc[:, G1:G1 + 1], None, ALU.mult).then_inc(z_scale, 1)
                    dve.wait_ge(z_rows, b * NC + (n + 1))
                    dve.wait_ge(s1_out, b * NC + (n + 2))
                    for k in range(CT):
                        nc.vector.tensor_tensor(raw[:, k, :], ps[:, 7, :], raw[:, k, :],
                                                ALU.mult).then_inc(y_scaled, 1)
                    dve.wait_ge(y_scaled, b * (NC * CT) + n * CT + CT)
                    for k in range(CT):
                        last = nc.vector.scalar_tensor_tensor(out=xs[:, k, cols(n)], in0=raw[:, k, :],
                                                              scalar=gbv[:, k:k + 1], in1=xs[:, k, cols(n)],
                                                              op0=ALU.add, op1=ALU.add)
                    last.then_inc(y_ready, 1)


def kernel(x, L0_conv_Wq, L0_conv_bq, L0_conv_Wk, L0_conv_bk, L0_conv_Wv, L0_conv_bv, L0_conv_Wo,
           L0_conv_bo, L0_conv_gamma, L1_conv_Wq, L1_conv_bq, L1_conv_Wk, L1_conv_bk, L1_conv_Wv,
           L1_conv_bv, L1_conv_gamma):
    import numpy as np
    import concourse.bacc as bacc
    from concourse import mybir as mb
    from concourse.bass_utils import run_bass_kernel_spmd

    def channels(w):
        return np.ascontiguousarray(np.asarray(w).T.reshape(CT, P, -1).transpose(1, 0, 2))

    f = np.float32
    a = {n: np.asarray(v) for n, v in locals().items() if n.startswith("L") or n == "x"}
    wq0, wk0 = a["L0_conv_Wq"], a["L0_conv_Wk"]
    wq1, wk1 = a["L1_conv_Wq"], a["L1_conv_Wk"]
    blank = np.zeros((2, C), f)
    percol = np.zeros((P, NPC), f)
    percol[:, BQ0] = np.concatenate([a["L0_conv_bq"]] * 2)
    percol[:, BK0] = np.concatenate([a["L0_conv_bk"]] * 2)
    percol[0:K1, BQ1] = np.concatenate([a["L1_conv_bq"]] * 3)
    percol[0:K1, BK1] = np.concatenate([a["L1_conv_bk"]] * 3)
    percol[K1:K1R, BK1] = 1.0
    percol[:, BO0:BO0 + CT] = a["L0_conv_bo"].reshape(CT, P).T
    percol[:, BV1:BV1 + CT] = a["L1_conv_bv"].reshape(CT, P).T
    percol[:, G0] = a["L0_conv_gamma"][0]
    percol[:, G1] = a["L1_conv_gamma"][0]
    arrays = {
        "x_in": np.ascontiguousarray(a["x"].reshape(BATCH, CT, P, N).transpose(0, 2, 1, 3)),
        "w_qk0": channels(np.concatenate([wq0, wq0, wk0, wk0])),
        "w_v0": channels(a["L0_conv_Wv"]),
        "w_o0": np.ascontiguousarray(np.concatenate([a["L0_conv_Wo"].T] * 2)),
        "b_v0": np.ascontiguousarray(np.broadcast_to(np.tile(a["L0_conv_bv"], TPC), (P, TPC * D0))),
        "w_qk1": channels(np.concatenate([wq1, wq1, wq1, blank, wk1, wk1, wk1, blank])),
        "w_v1": channels(a["L1_conv_Wv"]),
        "per_col": percol,
        "identity": np.eye(P, dtype=f),
    }
    nc = bacc.Bacc("TRN2", target_bir_lowering=False, num_devices=1)
    args = [nc.dram_tensor(n, v.shape, mb.dt.from_np(v.dtype), kind="ExternalInput").ap()
            for n, v in arrays.items()]
    y = nc.dram_tensor("y_out", (BATCH, P, CT, N), mb.dt.float32, kind="ExternalOutput").ap()
    build(nc, *args, y)
    r = run_bass_kernel_spmd(nc, [arrays], core_ids=[0])
    got = np.asarray(r.results[0]["y_out"])
    return np.ascontiguousarray(got.transpose(0, 2, 1, 3)).reshape(BATCH, C, 64, 64)
```

```python
import concourse.bass as bass
from concourse import mybir
from contextlib import ExitStack

F32 = mybir.dt.float32
F32R = mybir.dt.float32r
ALU = mybir.AluOpType
ACT = mybir.ActivationFunctionType
AX = mybir.AxisListType

P = 128
BATCH, C, N = 4, 256, 4096
CT = C // P
D0, D1 = C // 4, C // 8
NT = N // P
BANK = 512
NC = N // BANK
TPC = BANK // P

WIDE = 2048
HALVES = N // WIDE
MTILES = NT * HALVES

E0W = 1024
E0CH = N // E0W
STEPS0 = E0CH * NT
PAIRS = NT // 2
STEPS1 = NC * PAIRS

K1 = 3 * D1
K1R = K1 + 2
SLOTS = 4
LAG0 = 3
EBUF = 3

UNITS = TPC * NC
UNIT_AT = {2: range(0, 2)} | {u: range(2 + 3 * (u - 3), 2 + 3 * (u - 2)) for u in range(3, 13)}
ROWS_AT = 14

BQK0, BQK1, BO0, BV1, G0, G1, NPC = 0, 1, 2, 4, 6, 7, 8


def build(nc, x, wqk0, wv0, wo0, bv0, wqk1, wv1, percol, ident_d, out):
    ctx = ExitStack()
    with ctx:
        def sb(name, shape, dt):
            return ctx.enter_context(nc.sbuf_tensor(name, shape, dt))

        def sem(name):
            return ctx.enter_context(nc.semaphore(name))

        xs = sb("xs", [P, CT, N], F32)
        qs = sb("qs", [P, N], F32R)
        ks = sb("ks", [P, N], F32R)
        vs = sb("vs", [P, NT * 2 * C], F32R)
        v0 = vs[:, 0:NT * 2 * D0].rearrange("p (t h c) -> p t h c", t=NT, h=2)
        k0lo = vs[0:D0, N:2 * N]
        v1 = vs[:, :].rearrange("p (t h c) -> p t h c", t=NT, h=2)
        att = sb("att", [P, N], F32)
        zacc = att[:, 0:2 * BANK]
        raw = att[:, 2 * BANK:4 * BANK].rearrange("p (h n) -> p h n", h=CT)
        prob = sb("prob", [P, SLOTS, E0W], F32)
        phi = sb("phi", [P, SLOTS, E0W], F32R)
        plo = sb("plo", [P, SLOTS, E0W], F32R)
        vtmp = prob[:, 0, 0:TPC * D0]

        wqk0s = sb("wqk0s", [P, CT, 2 * D0], F32)
        wv0s = sb("wv0s", [P, CT, D0], F32)
        wo0s = sb("wo0s", [P, C], F32)
        bv0s = sb("bv0s", [P, TPC * D0], F32)
        wqk1s = sb("wqk1s", [P, CT, 2 * D1], F32)
        wv1s = sb("wv1s", [P, CT, C], F32)
        pc = sb("pc", [P, NPC], F32)
        ident = sb("ident", [P, P], F32)
        gbo = sb("gbo", [P, CT], F32)
        gbv = sb("gbv", [P, CT], F32)
        ones = sb("ones", [P, 1], F32)
        zeros = sb("zeros", [P, 2 * BANK], F32)
        rmax = sb("rmax", [P, MTILES], F32)
        sums = sb("sums", [P, STEPS0], F32)
        gmax = sb("gmax", [P, 1], F32)
        gmax_all = sb("gmax_all", [P, 1], F32)
        neg_max = sb("neg_max", [P, 1], F32)
        psum0 = sb("psum0", [P, 1], F32)
        psum0_all = sb("psum0_all", [P, 1], F32)
        rsum0 = sb("rsum0", [P, 1], F32)
        gscale0 = sb("gscale0", [P, 1], F32)
        unit_max = sb("unit_max", [P, TPC, NC], F32)
        row_max = sb("row_max", [P, TPC], F32)
        neg_rows = sb("neg_rows", [P, TPC, 2], F32R)
        qnext = sb("qnext", [K1, BANK], F32R)
        rz = sb("rz", [P, TPC], F32)
        rzg = sb("rzg", [P, TPC], F32)

        ps = ctx.enter_context(nc.psum_tensor("ps", [P, 8, BANK], F32))

        x_loaded = [sem(f"x_loaded{n}") for n in range(NC)]
        w_loaded = sem("w_loaded")
        consts_set = sem("consts_set")
        passed = sem("passed")
        out_stored = sem("out_stored")
        p0_qk = sem("p0_qk")
        p0_hi = sem("p0_hi")
        p0_v = sem("p0_v")
        p0_vt = sem("p0_vt")
        p0_vhi = sem("p0_vhi")
        p0_done = sem("p0_done")
        m_energy = sem("m_energy")
        m_free = sem("m_free")
        gmax_part = sem("gmax_part")
        gmax_full = sem("gmax_full")
        neg_set = sem("neg_set")
        x_biased = sem("x_biased")
        s0_energy = sem("s0_energy")
        s0_exp = sem("s0_exp")
        s0_hi = sem("s0_hi")
        s0_lo = sem("s0_lo")
        s0_av = sem("s0_av")
        s0_out = sem("s0_out")
        sum_part = sem("sum_part")
        sum_full = sem("sum_full")
        rsum_set = sem("rsum_set")
        scale_set = sem("scale_set")
        wo_done = sem("wo_done")
        x1_ready = sem("x1_ready")
        p1_qk = sem("p1_qk")
        p1_v = sem("p1_v")
        p1_hi = sem("p1_hi")
        p1_vhi = sem("p1_vhi")
        p1_lo = sem("p1_lo")
        p1_vlo = sem("p1_vlo")
        ones_set = sem("ones_set")
        unit_energy = sem("unit_energy")
        unit_free = sem("unit_free")
        qnext_set = sem("qnext_set")
        rows_max = sem("rows_max")
        rows_hi = sem("rows_hi")
        rows_lo = sem("rows_lo")
        rows_t = sem("rows_t")
        rows_in = sem("rows_in")
        s1_energy = sem("s1_energy")
        s1_exp = sem("s1_exp")
        s1_lo = sem("s1_lo")
        s1_sum = sem("s1_sum")
        s1_av = sem("s1_av")
        s1_out = sem("s1_out")
        z_part = sem("z_part")
        z_recip = sem("z_recip")
        z_scale = sem("z_scale")
        z_rows = sem("z_rows")
        y_scaled = sem("y_scaled")
        y_ready = sem("y_ready")

        def cols(n, w=BANK):
            return bass.ds(n * w, w)

        def settled(engine):
            engine.sem_inc(passed, 1)

        block = ctx.enter_context(nc.Block())

        @block.sync
        def _(sp):
            sp.dma_start(xs[:, :, 0:BANK], x[0, :, :, 0:BANK]).then_inc(x_loaded[0], 16)
            for dst, src in ((wqk0s, wqk0), (wv0s, wv0), (wo0s, wo0), (bv0s, bv0), (wqk1s, wqk1),
                             (wv1s, wv1), (pc, percol), (ident, ident_d)):
                sp.dma_start(dst[:], src).then_inc(w_loaded, 16)
            for n in range(1, NC):
                sp.dma_start(xs[:, :, n * BANK:(n + 1) * BANK],
                             x[0, :, :, n * BANK:(n + 1) * BANK]).then_inc(x_loaded[n], 16)
            with sp.Fori(0, BATCH - 1) as b:
                for n in range(NC):
                    c = slice(n * BANK, (n + 1) * BANK)
                    sp.wait_ge(y_ready, b * NC + (n + 2))
                    sp.dma_start(out[bass.ds(b, 1), :, :, c], xs[:, :, c]).then_inc(out_stored, 16)
                    sp.wait_ge(out_stored, b * (16 * NC) + 16 * (n + 1))
                    sp.dma_start(xs[:, :, c], x[bass.ds(b + 1, 1), :, :, c]).then_inc(x_loaded[n], 16)
            for n in range(NC):
                c = slice(n * BANK, (n + 1) * BANK)
                sp.wait_ge(y_ready, (BATCH - 1) * NC + n + 2)
                sp.dma_start(out[BATCH - 1, :, :, c], xs[:, :, c]).then_inc(out_stored, 16)
            sp.wait_ge(out_stored, 16 * NC * BATCH)

        @block.tensor
        def _(pe):
            mm = nc.tensor.matmul

            def project(dst, w, n):
                for c in range(CT):
                    last = mm(dst, w[:, c, :], xs[:, c, n * BANK:(n + 1) * BANK], start=c == 0, stop=c == CT - 1)
                return last

            def values(dst, w, n):
                for t in range(TPC):
                    for c in range(CT):
                        m = (n * TPC + t) * P
                        last = mm(dst(t), xs[:, c, m:m + P], w[:, c, :], start=c == 0, stop=c == CT - 1)
                return last

            def energy0(dst, t, n0):
                banks = dst.shape[1]
                for k in range(banks):
                    mm(dst[:, k, :], qs[:, t * P:(t + 1) * P], ks[:, bass.ds(n0 + k * BANK, BANK)],
                       start=True, stop=False)
                for k in range(banks):
                    last = mm(dst[:, k, :], qs[0:D0, t * P:(t + 1) * P],
                              k0lo[:, bass.ds(n0 + k * BANK, BANK)], start=False, stop=True)
                return last

            pe.wait_ge(w_loaded, 16 * 8)
            pe.sem_inc(s0_av, SLOTS)
            pe.sem_inc(s1_av, SLOTS)
            pe.sem_inc(z_part, 1)

            with pe.Fori(0, BATCH) as b:
                pe.wait_ge(y_ready, b * NC + 1)
                for n in range(NC):
                    pe.wait_ge(x_loaded[n], b * 16 + 16)
                    if n >= 2:
                        pe.wait_ge(p0_done, b * NC + (n - 1))
                    s = n % 2
                    project(ps[:, s, :], wqk0s, n).then_inc(p0_qk, 1)
                    values(lambda t: ps[:, 4 + s, t * D0:(t + 1) * D0], wv0s, n).then_inc(p0_v, 1)

                pe.wait_ge(p0_done, b * NC + NC)
                settled(pe)
                with pe.Fori(0, HALVES) as h:
                    for t in range(NT):
                        pe.wait_ge(m_free, b * MTILES + h * NT + (t + 1))
                        s = 4 * (t % 2)
                        energy0(ps[:, s:s + 4, :], t, h * WIDE).then_inc(m_energy, 1)

                pe.wait_ge(m_free, b * MTILES + (MTILES + 2))
                settled(pe)
                def energies0(t, h):
                    energy0(ps[:, 2 * (t % EBUF):2 * (t % EBUF) + 2, :], t, h * E0W).then_inc(s0_energy, 1)

                def attend0(t, h):
                    pe.wait_ge(s0_lo, b * STEPS0 + h * NT + (t + 1 + SLOTS))
                    if t == 0:
                        pe.wait_ge(s0_out, b * E0CH + h + 1)
                    for part in (phi, plo):
                        for k in range(E0W // BANK):
                            last = mm(ps[:, 6 + k, :], v0[:, t, :, :].rearrange("p h c -> p (h c)"),
                                      part[:, t % SLOTS, k * BANK:(k + 1) * BANK],
                                      start=t == 0 and part is phi, stop=t == NT - 1 and part is plo)
                    last.then_inc(s0_av, 1)

                def chunk0(h, final):
                    for t in range(NT):
                        ahead = t + LAG0
                        if ahead < NT or not final:
                            tile = ahead % NT
                            before = ahead - EBUF if ahead < NT else (NT - 1 - (NT - 1 - tile) % EBUF)
                            pe.wait_ge(s0_exp, b * STEPS0 + h * NT + (before + 1))
                            energies0(tile, h + 1 if ahead >= NT else h)
                        attend0(t, h)

                for t in range(LAG0):
                    energies0(t, 0)
                with pe.Fori(0, E0CH - 1) as h:
                    chunk0(h, False)
                chunk0(E0CH - 1, True)

                pe.wait_ge(s0_out, b * E0CH + (E0CH + 1))

                def project_out(n):
                    for k in range(CT):
                        last = mm(ps[:, k, :], wo0s[:, k * P:(k + 1) * P], att[:, n * BANK:(n + 1) * BANK],
                                  start=True, stop=True)
                    last.then_inc(wo_done, 1)

                def unit(k, chunk, weights, bank):
                    pe.wait_ge(unit_free, b * (NC * UNITS) + chunk * UNITS + (k + 1))
                    i, j = divmod(k, NC)
                    mm(ps[:, bank + k % 2, :], weights(i), ks[0:K1, j * BANK:(j + 1) * BANK],
                       start=True, stop=True).then_inc(unit_energy, 1)

                def first_units(j):
                    for i in range(TPC):
                        pe.wait_ge(unit_free, b * (NC * UNITS) + (j * TPC + i + 1))
                        mm(ps[:, 2 + i % 2, :], qs[0:K1, i * P:(i + 1) * P], ks[0:K1, j * BANK:(j + 1) * BANK],
                           start=True, stop=True).then_inc(unit_energy, 1)

                project_out(0)
                for n in range(NC):
                    pe.wait_ge(x1_ready, b * NC + (n + 1))
                    if n >= 2:
                        pe.wait_ge(p1_lo, b * NC + (n - 1))
                    project(ps[0:2 * D1, 4 + n % 2, :], wqk1s, n).then_inc(p1_qk, 1)
                    if n + 1 < NC:
                        project_out(n + 1)
                    if n >= 1:
                        pe.wait_ge(p1_vlo, b * NC + n)
                    values(lambda t: ps[:, 6 + t // 2, (t % 2) * C:(t % 2 + 1) * C], wv1s, n).then_inc(p1_v, 1)
                    if n >= 1:
                        pe.wait_ge(p1_lo, b * NC + n)
                        first_units(n - 1)
                pe.wait_ge(p1_lo, b * NC + NC)
                first_units(NC - 1)

                def turn_rows(n):
                    pe.wait_ge(rows_lo, b * NC + n + 1)
                    for q in range(TPC):
                        last = mm(ps[0:2, 7, q * P:(q + 1) * P], neg_rows[:, q, :].bitcast(F32), ident[:],
                                  start=True, stop=True)
                    last.then_inc(rows_t, 1)

                def energies1(u, n):
                    for j in range(2):
                        t = 2 * u + j
                        last = mm(ps[:, 2 * (u % 2) + j, :], ks[0:K1R, t * P:(t + 1) * P],
                                  qs[0:K1R, cols(n)], start=True, stop=True)
                    last.then_inc(s1_energy, 1)

                def chunk1(n, final):
                    for u in range(PAIRS):
                        if u == ROWS_AT and not final:
                            turn_rows(n + 1)
                        if u + 1 < PAIRS or not final:
                            pe.wait_ge(s1_exp, b * (2 * STEPS1) + n * (2 * PAIRS) + (2 * u + 2))
                            if u + 1 == PAIRS:
                                pe.wait_ge(rows_in, b * NC + n + 2)
                            energies1((u + 1) % PAIRS, n + 1 if u + 1 == PAIRS else n)
                        if u == PAIRS - 1:
                            pe.wait_ge(s1_sum, b * STEPS1 + n * PAIRS + (PAIRS + SLOTS))
                            for q in range(TPC):
                                for j in range(2):
                                    last = mm(ps[:, 6, q:q + 1],
                                              zacc[:, j * BANK + q * P:j * BANK + (q + 1) * P], ones[:],
                                              start=j == 0, stop=j == 1)
                            last.then_inc(z_part, 1)
                        units = [] if final else list(UNIT_AT.get(u, ()))
                        if units and u == min(UNIT_AT):
                            pe.wait_ge(qnext_set, b * (NC - 1) + n + 1)
                            pe.wait_ge(y_scaled, b * NC + n + 1)
                        pe.wait_ge(s1_exp, b * (2 * STEPS1) + n * (2 * PAIRS) + (2 * u + 2 + 2))
                        if u == 0:
                            pe.wait_ge(s1_out, b * NC + n + 1)
                        for part, lo in ((phi, 0), (phi, 1), (plo, 0)):
                            if part is plo:
                                pe.wait_ge(s1_lo, b * STEPS1 + n * PAIRS + (u + 1 + SLOTS))
                            for j in range(2):
                                for k in range(CT):
                                    last = mm(ps[:, 4 + k, :], v1[:, 2 * u + j, lo, k * P:(k + 1) * P],
                                              part[:, u % SLOTS, j * BANK:(j + 1) * BANK],
                                              start=u == 0 and j == 0 and part is phi and lo == 0,
                                              stop=u == PAIRS - 1 and j == 1 and part is plo)
                            if part is plo:
                                last.then_inc(s1_av, 1)
                            if units:
                                unit(units.pop(0), n + 1, lambda i: qnext[:, i * P:(i + 1) * P], 6)
                    pe.wait_ge(z_scale, b * NC + n + 1)
                    for q in range(TPC):
                        last = mm(ps[:, 7, q * P:(q + 1) * P], rzg[:, q:q + 1].to_broadcast([P, P]), ident[:],
                                  start=True, stop=True)
                    last.then_inc(z_rows, 1)

                pe.wait_ge(p1_vlo, b * NC + NC)
                turn_rows(0)
                pe.wait_ge(rows_in, b * NC + 1)
                pe.wait_ge(ones_set, b + 1)
                energies1(0, 0)
                with pe.Fori(0, NC - 1) as n:
                    chunk1(n, False)
                chunk1(NC - 1, True)

        @block.scalar
        def _(act):
            act.sem_inc(s1_exp, 2)
            act.sem_inc(s0_out, 1)
            act.sem_inc(s1_out, 1)
            act.wait_ge(w_loaded, 16 * 8)
            with act.Fori(0, BATCH) as b:
                for n in range(NC):
                    c = slice(n * BANK, (n + 1) * BANK)
                    s = n % 2
                    act.wait_ge(p0_qk, b * NC + (n + 1))
                    nc.scalar.activation(qs[0:D0, c], ps[0:D0, s, :], ACT.Identity,
                                         bias=pc[0:D0, BQK0:BQK0 + 1])
                    for half in (0, D0):
                        last = nc.scalar.activation(ks[half:half + D0, c], ps[D0:P, s, :], ACT.Identity,
                                                    bias=pc[D0:P, BQK0:BQK0 + 1])
                    last.then_inc(p0_hi, 1)
                    act.wait_ge(p0_vt, b * NC + (n + 1))
                    nc.scalar.copy(v0[:, n * TPC:(n + 1) * TPC, 0, :],
                                   vtmp.rearrange("p (t c) -> p t c", t=TPC)).then_inc(p0_vhi, 1)
                act.wait_ge(p0_done, b * NC + NC)
                act.wait_ge(consts_set, 3)
                for k in range(CT):
                    nc.scalar.activation(xs[:, k, :], xs[:, k, :], ACT.Identity,
                                         bias=gbo[:, k:k + 1]).then_inc(x_biased, 1)
                act.wait_ge(gmax_full, b + 1)
                nc.scalar.mul(neg_max[:], gmax_all[:], -1.0).then_inc(neg_set, 1)
                act.wait_ge(neg_set, b + 1)

                def exp0(t, h):
                    act.wait_ge(s0_energy, b * STEPS0 + h * NT + (t + 1))
                    act.wait_ge(s0_lo, b * STEPS0 + h * NT + (t + 1))
                    s = 2 * (t % NT % EBUF)
                    nc.scalar.activation(prob[:, t % SLOTS, :].rearrange("p (k n) -> p k n", k=2),
                                         ps[:, s:s + 2, :], ACT.Exp, bias=neg_max[:],
                                         accum_out=sums[:, bass.ds(h * NT + t, 1)]).then_inc(s0_exp, 1)

                def move_out0(h):
                    act.wait_ge(s0_av, b * STEPS0 + h * NT + (NT + SLOTS))
                    nc.scalar.copy(att[:, bass.ds(h * E0W, E0W)].rearrange("p (k n) -> p k n", k=2),
                                   ps[:, 6:8, :]).then_inc(s0_out, 1)

                for t in range(LAG0):
                    exp0(t, 0)
                with act.Fori(0, E0CH - 1) as h:
                    for t in range(LAG0, NT + LAG0):
                        exp0(t, h)
                    move_out0(h)
                for t in range(LAG0, NT):
                    exp0(t, E0CH - 1)
                move_out0(E0CH - 1)

                for n in range(NC):
                    c = slice(n * BANK, (n + 1) * BANK)
                    act.wait_ge(p1_qk, b * NC + (n + 1))
                    for dst, rows, src in ((qs, 0, 0), (qs, 2, 0), (ks, 0, 1), (ks, 1, 1)):
                        last = nc.scalar.activation(dst[rows * D1:(rows + 1) * D1, c],
                                                    ps[src * D1:(src + 1) * D1, 4 + n % 2, :], ACT.Identity,
                                                    bias=pc[src * D1:(src + 1) * D1, BQK1:BQK1 + 1])
                    last.then_inc(p1_hi, 1)
                    act.wait_ge(p1_v, b * NC + (n + 1))
                    nc.scalar.copy(v1[:, n * TPC:(n + 1) * TPC, 0, :],
                                   ps[:, 6:8, :].rearrange("p k (t c) -> p (k t) c", c=C)).then_inc(p1_vhi, 1)

                def insert_rows(n):
                    act.wait_ge(rows_t, b * NC + n + 1)
                    nc.scalar.copy(qs[K1:K1R, cols(n)], ps[0:2, 7, :]).then_inc(rows_in, 1)

                def exp1(u, n):
                    act.wait_ge(s1_energy, b * STEPS1 + n * PAIRS + (u + 1))
                    act.wait_ge(s1_lo, b * STEPS1 + n * PAIRS + (u + 1))
                    act.wait_ge(s1_sum, b * STEPS1 + n * PAIRS + (u + 1))
                    s = 2 * (u % 2)
                    nc.scalar.activation(prob[:, u % SLOTS, :].rearrange("p (k n) -> p k n", k=2),
                                         ps[:, s:s + 2, :], ACT.Exp).then_inc(s1_exp, 1)
                    act.wait_ge(s1_av, b * STEPS1 + n * PAIRS + (u + 1))
                    nc.scalar.activation(phi[:, u % SLOTS, :].rearrange("p (k n) -> p k n", k=2),
                                         ps[:, s:s + 2, :], ACT.Exp).then_inc(s1_exp, 1)

                def chunk1(n, final):
                    for u in range(PAIRS):
                        if u + 1 < PAIRS or not final:
                            exp1(u + 1, n)
                        if u == ROWS_AT and not final:
                            insert_rows(n + 1)
                    act.wait_ge(s1_av, b * STEPS1 + n * PAIRS + (PAIRS + SLOTS))
                    nc.scalar.copy(raw, ps[:, 4:6, :]).then_inc(s1_out, 1)

                insert_rows(0)
                exp1(0, 0)
                with act.Fori(0, NC - 1) as n:
                    chunk1(n, False)
                chunk1(NC - 1, True)

        @block.gpsimd
        def _(pool):
            pool.wait_ge(consts_set, 1)
            pool.sem_inc(s1_sum, SLOTS)
            with pool.Fori(0, BATCH) as b:
                pool.wait_ge(gmax_part, b + 1)
                settled(pool)
                nc.gpsimd.partition_all_reduce(gmax_all[:], gmax[:], P,
                                               bass.bass_isa.ReduceOp.max).then_inc(gmax_full, 1)
                with pool.Fori(0, E0CH) as h:
                    for t in range(NT):
                        pool.wait_ge(s0_exp, b * STEPS0 + h * NT + (t + 1))
                        pool.wait_ge(s0_av, b * STEPS0 + h * NT + (t + 1))
                        settled(pool)
                        nc.gpsimd.tensor_scalar(phi[:, t % SLOTS, :], prob[:, t % SLOTS, :], 1.0, 0.0,
                                                ALU.mult, ALU.add).then_inc(s0_hi, 1)
                pool.wait_ge(s0_av, b * STEPS0 + (STEPS0 + SLOTS))
                settled(pool)
                nc.gpsimd.memset(ks[K1:K1R, :].bitcast(F32), 1.0).then_inc(ones_set, 1)
                pool.wait_ge(sum_part, b + 1)
                pool.wait_ge(ones_set, b + 1)
                settled(pool)
                nc.gpsimd.partition_all_reduce(psum0_all[:], psum0[:], P,
                                               bass.bass_isa.ReduceOp.add).then_inc(sum_full, 1)
                with pool.Fori(0, NC) as n:
                    pool.wait_ge(z_part, b * NC + (n + 1))
                    for u in range(PAIRS):
                        pool.wait_ge(s1_exp, b * (2 * STEPS1) + n * (2 * PAIRS) + (2 * u + 1 + 2))
                        if u >= 1:
                            pool.wait_ge(s1_sum, b * STEPS1 + n * PAIRS + (u + SLOTS))
                        nc.gpsimd.tensor_tensor(zacc, zacc if u else zeros[:], prob[:, u % SLOTS, :],
                                                ALU.add).then_inc(s1_sum, 1)

        @block.vector
        def _(dve):
            nc.vector.memset(zeros[:], 0.0).then_inc(consts_set, 1)
            nc.vector.memset(ones[:], 1.0)
            dve.sem_inc(m_free, 2)
            dve.sem_inc(s0_lo, SLOTS)
            dve.sem_inc(s1_lo, SLOTS)
            dve.sem_inc(unit_free, 2)
            dve.sem_inc(y_scaled, 1)
            dve.sem_inc(y_ready, 1)
            dve.wait_ge(w_loaded, 16 * 8)
            nc.vector.tensor_scalar(gbo[:], pc[:, BO0:BO0 + CT], pc[:, G0:G0 + 1], None,
                                    ALU.mult).then_inc(consts_set, 1)
            nc.vector.tensor_scalar(gbv[:], pc[:, BV1:BV1 + CT], pc[:, G1:G1 + 1], None,
                                    ALU.mult).then_inc(consts_set, 1)
            with dve.Fori(0, BATCH) as b:
                def low(out, src, bias, hi):
                    return nc.vector.scalar_tensor_tensor(out=out, in0=src, scalar=bias, in1=hi.bitcast(F32),
                                                          op0=ALU.add, op1=ALU.subtract)

                for n in range(NC):
                    c = slice(n * BANK, (n + 1) * BANK)
                    s = n % 2
                    dve.wait_ge(p0_hi, b * NC + (n + 1))
                    low(qs[D0:P, c], ps[0:D0, s, :], pc[0:D0, BQK0:BQK0 + 1], qs[0:D0, c])
                    low(k0lo[:, c], ps[D0:P, s, :], pc[D0:P, BQK0:BQK0 + 1], ks[D0:P, c])
                    dve.wait_ge(p0_v, b * NC + (n + 1))
                    if n >= 1:
                        dve.wait_ge(p0_done, b * NC + n)
                    nc.vector.tensor_tensor(vtmp, ps[:, 4 + s, 0:TPC * D0], bv0s[:], ALU.add).then_inc(p0_vt, 1)
                    dve.wait_ge(p0_vhi, b * NC + (n + 1))
                    nc.vector.tensor_tensor(v0[:, n * TPC:(n + 1) * TPC, 1, :],
                                            vtmp.rearrange("p (t c) -> p t c", t=TPC),
                                            v0[:, n * TPC:(n + 1) * TPC, 0, :].bitcast(F32),
                                            ALU.subtract).then_inc(p0_done, 1)

                with dve.Fori(0, HALVES) as h:
                    for t in range(NT):
                        dve.wait_ge(m_energy, b * MTILES + h * NT + (t + 1))
                        s = 4 * (t % 2)
                        nc.vector.tensor_reduce(rmax[:, bass.ds(h * NT + t, 1)], ps[:, s:s + 4, :], AX.XY,
                                                ALU.max).then_inc(m_free, 1)
                dve.wait_ge(m_free, b * MTILES + (MTILES + 2))
                nc.vector.tensor_reduce(gmax[:], rmax[:], AX.X, ALU.max).then_inc(gmax_part, 1)

                with dve.Fori(0, E0CH) as h:
                    for t in range(NT):
                        dve.wait_ge(s0_hi, b * STEPS0 + h * NT + (t + 1))
                        nc.vector.tensor_tensor(plo[:, t % SLOTS, :], prob[:, t % SLOTS, :],
                                                phi[:, t % SLOTS, :].bitcast(F32),
                                                ALU.subtract).then_inc(s0_lo, 1)
                dve.wait_ge(s0_exp, b * STEPS0 + STEPS0)
                nc.vector.tensor_reduce(psum0[:], sums[:], AX.X, ALU.add).then_inc(sum_part, 1)
                dve.wait_ge(sum_full, b + 1)
                nc.vector.reciprocal(rsum0[:], psum0_all[:]).then_inc(rsum_set, 1)
                dve.wait_ge(rsum_set, b + 1)
                nc.vector.tensor_scalar(gscale0[:], rsum0[:], pc[:, G0:G0 + 1], None,
                                        ALU.mult).then_inc(scale_set, 1)
                dve.wait_ge(scale_set, b + 1)
                dve.wait_ge(x_biased, b * CT + CT)

                def input1(n):
                    c = slice(n * BANK, (n + 1) * BANK)
                    dve.wait_ge(wo_done, b * NC + (n + 1))
                    nc.vector.scalar_tensor_tensor(out=xs[:, :, c], in0=ps[:, 0:2, :], scalar=gscale0[:],
                                                   in1=xs[:, :, c], op0=ALU.mult, op1=ALU.add).then_inc(x1_ready, 1)

                def reduce_unit(k, chunk, i, j, bank):
                    dve.wait_ge(unit_energy, b * (NC * UNITS) + chunk * UNITS + (k + 1))
                    nc.vector.tensor_reduce(unit_max[:, i, j:j + 1], ps[:, bank + k % 2, :], AX.X,
                                            ALU.max).then_inc(unit_free, 1)

                input1(0)
                for n in range(NC):
                    c = slice(n * BANK, (n + 1) * BANK)
                    dve.wait_ge(p1_hi, b * NC + (n + 1))
                    low(qs[D1:2 * D1, c], ps[0:D1, 4 + n % 2, :], pc[0:D1, BQK1:BQK1 + 1], qs[0:D1, c])
                    low(ks[2 * D1:K1, c], ps[D1:2 * D1, 4 + n % 2, :], pc[D1:2 * D1, BQK1:BQK1 + 1],
                        ks[D1:2 * D1, c]).then_inc(p1_lo, 1)
                    if n + 1 < NC:
                        input1(n + 1)
                    if n >= 1:
                        for i in range(TPC):
                            reduce_unit((n - 1) * TPC + i, 0, i, n - 1, 2)
                    dve.wait_ge(p1_vhi, b * NC + (n + 1))
                    nc.vector.tensor_tensor(v1[:, n * TPC:(n + 1) * TPC, 1, :],
                                            ps[:, 6:8, :].rearrange("p k (t c) -> p (k t) c", c=C),
                                            v1[:, n * TPC:(n + 1) * TPC, 0, :].bitcast(F32),
                                            ALU.subtract).then_inc(p1_vlo, 1)
                for i in range(TPC):
                    reduce_unit((NC - 1) * TPC + i, 0, i, NC - 1, 2)

                def split_rows(n):
                    dve.wait_ge(unit_free, b * (NC * UNITS) + n * UNITS + (UNITS + 2))
                    nc.vector.tensor_reduce(row_max[:], unit_max[:], AX.X, ALU.max).then_inc(rows_max, 1)
                    dve.wait_ge(rows_max, b * NC + n + 1)
                    nc.vector.tensor_scalar(neg_rows[:, :, 0], row_max[:], -1.0, None,
                                            ALU.mult).then_inc(rows_hi, 1)
                    dve.wait_ge(rows_hi, b * NC + n + 1)
                    nc.vector.scalar_tensor_tensor(out=neg_rows[:, :, 1], in0=row_max[:], scalar=-1.0,
                                                   in1=neg_rows[:, :, 0].bitcast(F32), op0=ALU.mult,
                                                   op1=ALU.subtract).then_inc(rows_lo, 1)

                def low1(u, n):
                    dve.wait_ge(s1_exp, b * (2 * STEPS1) + n * (2 * PAIRS) + (2 * u + 2 + 2))
                    nc.vector.tensor_tensor(plo[:, u % SLOTS, :], prob[:, u % SLOTS, :],
                                            phi[:, u % SLOTS, :].bitcast(F32),
                                            ALU.subtract).then_inc(s1_lo, 1)

                def chunk1(n, final):
                    if not final:
                        nc.vector.tensor_copy(qnext[:], qs[0:K1, cols(n + 1)]).then_inc(qnext_set, 1)
                    for u in range(PAIRS):
                        if u == PAIRS - 1:
                            dve.wait_ge(z_part, b * NC + n + 2)
                            nc.vector.reciprocal(rz[:], ps[:, 6, 0:TPC]).then_inc(z_recip, 1)
                            dve.wait_ge(z_recip, b * NC + n + 1)
                            nc.vector.tensor_scalar(rzg[:], rz[:], pc[:, G1:G1 + 1], None,
                                                    ALU.mult).then_inc(z_scale, 1)
                        if u + 1 < PAIRS or not final:
                            low1(u + 1, n)
                        if not final:
                            for k in UNIT_AT.get(u, ()):
                                reduce_unit(k, n + 1, *divmod(k, NC), 6)
                            if u == max(UNIT_AT):
                                split_rows(n + 1)
                    dve.wait_ge(z_rows, b * NC + n + 1)
                    dve.wait_ge(s1_out, b * NC + n + 2)
                    for k in range(CT):
                        last = nc.vector.tensor_tensor(raw[:, k, :], ps[:, 7, :], raw[:, k, :], ALU.mult)
                    last.then_inc(y_scaled, 1)
                    dve.wait_ge(y_scaled, b * NC + n + 2)
                    for k in range(CT):
                        last = nc.vector.scalar_tensor_tensor(out=xs[:, k, cols(n)], in0=raw[:, k, :],
                                                              scalar=gbv[:, k:k + 1], in1=xs[:, k, cols(n)],
                                                              op0=ALU.add, op1=ALU.add)
                    last.then_inc(y_ready, 1)

                split_rows(0)
                low1(0, 0)
                with dve.Fori(0, NC - 1) as n:
                    chunk1(n, False)
                chunk1(NC - 1, True)


def kernel(x, L0_conv_Wq, L0_conv_bq, L0_conv_Wk, L0_conv_bk, L0_conv_Wv, L0_conv_bv, L0_conv_Wo,
           L0_conv_bo, L0_conv_gamma, L1_conv_Wq, L1_conv_bq, L1_conv_Wk, L1_conv_bk, L1_conv_Wv,
           L1_conv_bv, L1_conv_gamma):
    import numpy as np
    import concourse.bacc as bacc
    from concourse import mybir as mb
    from concourse.bass_utils import run_bass_kernel_spmd

    def channels(w):
        return np.ascontiguousarray(np.asarray(w).T.reshape(CT, P, -1).transpose(1, 0, 2))

    f = np.float32
    a = {n: np.asarray(v) for n, v in locals().items() if n.startswith("L") or n == "x"}
    wq0, wk0 = a["L0_conv_Wq"], a["L0_conv_Wk"]
    wq1, wk1 = a["L1_conv_Wq"], a["L1_conv_Wk"]
    percol = np.zeros((P, NPC), f)
    percol[:, BQK0] = np.concatenate([a["L0_conv_bq"], a["L0_conv_bk"]])
    percol[0:2 * D1, BQK1] = np.concatenate([a["L1_conv_bq"], a["L1_conv_bk"]])
    percol[:, BO0:BO0 + CT] = a["L0_conv_bo"].reshape(CT, P).T
    percol[:, BV1:BV1 + CT] = a["L1_conv_bv"].reshape(CT, P).T
    percol[:, G0] = a["L0_conv_gamma"][0]
    percol[:, G1] = a["L1_conv_gamma"][0]
    arrays = {
        "x_in": np.ascontiguousarray(a["x"].reshape(BATCH, CT, P, N).transpose(0, 2, 1, 3)),
        "w_qk0": channels(np.concatenate([wq0, wk0])),
        "w_v0": channels(a["L0_conv_Wv"]),
        "w_o0": np.ascontiguousarray(np.concatenate([a["L0_conv_Wo"].T] * 2)),
        "b_v0": np.ascontiguousarray(np.broadcast_to(np.tile(a["L0_conv_bv"], TPC), (P, TPC * D0))),
        "w_qk1": channels(np.concatenate([wq1, wk1])),
        "w_v1": channels(a["L1_conv_Wv"]),
        "per_col": percol,
        "identity": np.eye(P, dtype=f),
    }
    nc = bacc.Bacc("TRN2", target_bir_lowering=False, num_devices=1)
    args = [nc.dram_tensor(n, v.shape, mb.dt.from_np(v.dtype), kind="ExternalInput").ap()
            for n, v in arrays.items()]
    y = nc.dram_tensor("y_out", (BATCH, P, CT, N), mb.dt.float32, kind="ExternalOutput").ap()
    build(nc, *args, y)
    r = run_bass_kernel_spmd(nc, [arrays], core_ids=[0])
    got = np.asarray(r.results[0]["y_out"])
    return np.ascontiguousarray(got.transpose(0, 2, 1, 3)).reshape(BATCH, C, 64, 64)
```

```python
import concourse.bass as bass
from concourse import mybir
from contextlib import ExitStack

F32 = mybir.dt.float32
F32R = mybir.dt.float32r
ALU = mybir.AluOpType
ACT = mybir.ActivationFunctionType
AX = mybir.AxisListType

P = 128
BATCH, C, N = 4, 256, 4096
CT = C // P
D0, D1 = C // 4, C // 8
NT = N // P
BANK = 512
NC = N // BANK
TPC = BANK // P

WIDE = 1024
WIDES = N // WIDE
TPW = WIDE // P
CPW = WIDE // BANK
MTILES = NT * WIDES
MBUF = 3
LOW_DVE = 4

QK_HI, QK_LO, VALUES, TURN = range(4)


def order_of_maxima():
    steps = [("project", 0, QK_HI), ("project", 0, QK_LO), ("project", 1, QK_HI), ("project", 1, QK_LO),
             ("low", 0), ("low", 1)]
    count = 0
    for p in range(WIDES):
        tiles = [(t, p) for t in range((p + 1) * TPW)]
        tiles += [(t, q) for q in range(p) for t in range(p * TPW, (p + 1) * TPW)]
        todo = []
        for n in range((p + 1) * CPW, (p + 2) * CPW if p + 1 < WIDES else NC + 3):
            todo += [(n, QK_HI), (n, QK_LO), (n - 3, TURN), (n - 2, VALUES)]
        todo = [("project", n, i) for n, i in todo if 0 <= n < NC]
        spread = len(tiles) - (3 if p == 0 else 8)
        done = 0
        behind = []
        for i, (t, q) in enumerate(tiles):
            steps.append(("max", count, t, q))
            count += 1
            for due in [d for d in behind if d[1] <= i]:
                steps.append(("low", due[0]))
                behind.remove(due)
            while done < len(todo) and done * spread < (i + 1) * len(todo):
                step = todo[done]
                done += 1
                if step[2] == QK_HI:
                    steps += [("low", d[0]) for d in behind]
                    behind = []
                steps.append(step)
                if step[2] == QK_LO:
                    behind.append((step[1], i + 2))
        steps += [("low", d[0]) for d in behind]
    return steps


def qk_bank(n):
    return 1 if n == 1 else 0


E0W = 1024
E0CH = N // E0W
STEPS0 = E0CH * NT
PAIRS = NT // 2
STEPS1 = NC * PAIRS

K1 = 3 * D1
K1R = K1 + 2
SLOTS = 4
XBUF = SLOTS
LAG0 = 3
EBUF = 3

UNITS = TPC * NC
UNIT_AT = {2: range(0, 2)} | {u: range(2 + 3 * (u - 3), 2 + 3 * (u - 2)) for u in range(3, 13)}
ROWS_AT = 14

BQK0, BQK1, BO0, BV1, G0, G1, BV0, NPC = 0, 1, 2, 4, 6, 7, 8, 9

WQK0, WV0 = 0, CT * 2 * D0
WQK1 = WV0 + CT * 2 * D0
WV1 = WQK1 + CT * 2 * D1
WALL = WV1 + CT * C


def build(nc, x, weights, wo0, percol, ident_d, out):
    ctx = ExitStack()
    with ctx:
        def sb(name, shape, dt):
            return ctx.enter_context(nc.sbuf_tensor(name, shape, dt))

        def sem(name):
            return ctx.enter_context(nc.semaphore(name))

        xs = sb("xs", [P, CT, N], F32)
        qs = sb("qs", [P, N], F32R)
        ks = sb("ks", [P, N], F32R)
        vs = sb("vs", [P, NT * 2 * C], F32R)
        v0 = vs[:, 0:NT * 2 * D0].rearrange("p (t h c) -> p t h c", t=NT, h=2)
        k0lo = vs[0:D0, N:2 * N]
        v1 = vs[:, :].rearrange("p (t h c) -> p t h c", t=NT, h=2)
        att = sb("att", [P, N], F32)
        zacc = att[:, 0:2 * BANK]
        raw = att[:, 2 * BANK:4 * BANK].rearrange("p (h n) -> p h n", h=CT)
        prob = sb("prob", [P, SLOTS, E0W], F32)
        phi = sb("phi", [P, SLOTS, E0W], F32R)
        plo = sb("plo", [P, SLOTS, E0W], F32R)
        xhi = phi[:, :, :].rearrange("p s (k n) -> p s k n", k=CT)
        xlo = plo[:, :, :].rearrange("p s (k n) -> p s k n", k=CT)
        vtmp = prob[:, 0:2, 0:BANK]
        qktmp = prob[:, 2:4, 0:BANK]
        vstack = vs[:, 2 * N:2 * N + 2 * BANK].rearrange("p (s n) -> p s n", s=2)
        wraw = prob[:, :, :].rearrange("p s n -> p (s n)")[:, 0:WALL]

        w_hi = sb("w_hi", [P, WALL], F32R)
        w_lo = sb("w_lo", [P, WALL], F32R)
        wo0s = sb("wo0s", [P, C], F32)
        pc = sb("pc", [P, NPC], F32)
        ident = sb("ident", [P, P], F32)
        ident_r = sb("ident_r", [P, P], F32R)
        gbo = sb("gbo", [P, CT], F32)
        gbv = sb("gbv", [P, CT], F32)
        ones = sb("ones", [P, 1], F32)
        rmax = sb("rmax", [P, MTILES], F32)
        sums = sb("sums", [P, STEPS0], F32)
        gmax = sb("gmax", [P, 1], F32)
        gmax_all = sb("gmax_all", [P, 1], F32)
        neg_max = sb("neg_max", [P, 1], F32)
        psum0 = sb("psum0", [P, 1], F32)
        psum0_all = sb("psum0_all", [P, 1], F32)
        rsum0 = sb("rsum0", [P, 1], F32)
        gscale0 = sb("gscale0", [P, 1], F32)
        unit_max = sb("unit_max", [P, TPC, NC], F32)
        row_max = sb("row_max", [P, TPC], F32)
        neg_rows = sb("neg_rows", [P, TPC, 2], F32R)
        qnext = sb("qnext", [K1, BANK], F32R)
        rz = sb("rz", [P, TPC], F32)
        rzg = sb("rzg", [P, TPC], F32)

        ps = ctx.enter_context(nc.psum_tensor("ps", [P, 8, BANK], F32))

        x_loaded = [sem(f"x_loaded{n}") for n in range(NC)]
        w_loaded = sem("w_loaded")
        w_rounded = sem("w_rounded")
        w_split = sem("w_split")
        consts_set = sem("consts_set")
        passed = sem("passed")
        out_stored = sem("out_stored")
        p0_qk = sem("p0_qk")
        p0_v = sem("p0_v")
        p0_hi = sem("p0_hi")
        p0_lo = sem("p0_lo")
        p0_qlo = sem("p0_qlo")
        p0_lo_pool = sem("p0_lo_pool")
        p0_vhi = sem("p0_vhi")
        p0_vlo = sem("p0_vlo")
        p0_turned = sem("p0_turned")
        p0_vout = sem("p0_vout")
        p0_xhi = sem("p0_xhi")
        p0_xlo_first = sem("p0_xlo_first")
        p0_xlo = sem("p0_xlo")
        m_energy = sem("m_energy")
        m_free = sem("m_free")
        gmax_full = sem("gmax_full")
        neg_set = sem("neg_set")
        x_biased = sem("x_biased")
        s0_energy = sem("s0_energy")
        s0_exp = sem("s0_exp")
        s0_hi = sem("s0_hi")
        s0_lo = sem("s0_lo")
        s0_av = sem("s0_av")
        s0_out = sem("s0_out")
        sum_part = sem("sum_part")
        sum_full = sem("sum_full")
        rsum_set = sem("rsum_set")
        scale_set = sem("scale_set")
        wo_done = sem("wo_done")
        x1_ready = sem("x1_ready")
        p1_xhi = sem("p1_xhi")
        p1_xlo = sem("p1_xlo")
        p1_qk = sem("p1_qk")
        p1_v = sem("p1_v")
        p1_hi = sem("p1_hi")
        p1_vhi = sem("p1_vhi")
        p1_lo = sem("p1_lo")
        p1_vlo = sem("p1_vlo")
        ones_set = sem("ones_set")
        unit_energy = sem("unit_energy")
        unit_free = sem("unit_free")
        qnext_set = sem("qnext_set")
        rows_max = sem("rows_max")
        rows_hi = sem("rows_hi")
        rows_lo = sem("rows_lo")
        rows_t = sem("rows_t")
        rows_in = sem("rows_in")
        s1_energy = sem("s1_energy")
        s1_exp = sem("s1_exp")
        s1_lo = sem("s1_lo")
        s1_sum = sem("s1_sum")
        s1_av = sem("s1_av")
        s1_out = sem("s1_out")
        z_part = sem("z_part")
        z_sum = sem("z_sum")
        z_recip = sem("z_recip")
        z_scale = sem("z_scale")
        z_rows = sem("z_rows")
        y_scaled = sem("y_scaled")
        y_ready = sem("y_ready")

        def cols(n, w=BANK):
            return bass.ds(n * w, w)

        def settled(engine):
            engine.sem_inc(passed, 1)

        ORDER0 = order_of_maxima()
        block = ctx.enter_context(nc.Block())

        @block.sync
        def _(sp):
            sp.dma_start(xs[:, :, 0:BANK], x[0, :, :, 0:BANK]).then_inc(x_loaded[0], 16)
            sp.dma_start(wraw, weights).then_inc(w_loaded, 16)
            for dst, src in ((pc, percol), (ident, ident_d), (wo0s, wo0)):
                sp.dma_start(dst[:], src).then_inc(w_loaded, 16)
            for n in range(1, NC):
                sp.dma_start(xs[:, :, n * BANK:(n + 1) * BANK],
                             x[0, :, :, n * BANK:(n + 1) * BANK]).then_inc(x_loaded[n], 16)
            with sp.Fori(0, BATCH - 1) as b:
                for n in range(NC):
                    c = slice(n * BANK, (n + 1) * BANK)
                    sp.wait_ge(y_ready, b * NC + (n + 2))
                    sp.dma_start(out[bass.ds(b, 1), :, :, c], xs[:, :, c]).then_inc(out_stored, 16)
                    sp.wait_ge(out_stored, b * (16 * NC) + 16 * (n + 1))
                    sp.dma_start(xs[:, :, c], x[bass.ds(b + 1, 1), :, :, c]).then_inc(x_loaded[n], 16)
            for n in range(NC):
                c = slice(n * BANK, (n + 1) * BANK)
                sp.wait_ge(y_ready, (BATCH - 1) * NC + n + 2)
                sp.dma_start(out[BATCH - 1, :, :, c], xs[:, :, c]).then_inc(out_stored, 16)
            sp.wait_ge(out_stored, 16 * NC * BATCH)

        @block.tensor
        def _(pe):
            mm = nc.tensor.matmul

            def energy0(dst, t, n0):
                for k in range(2):
                    mm(dst[:, k, :], qs[:, t * P:(t + 1) * P], ks[:, bass.ds(n0 + k * BANK, BANK)],
                       start=True, stop=False)
                for k in range(2):
                    last = mm(dst[:, k, :], qs[0:D0, t * P:(t + 1) * P],
                              k0lo[:, bass.ds(n0 + k * BANK, BANK)], start=False, stop=True)
                return last

            pe.wait_ge(consts_set, 1)
            pe.wait_ge(w_loaded, 16 * 4)
            pe.wait_ge(w_split, 1)
            pe.sem_inc(s0_av, SLOTS)
            pe.sem_inc(s1_av, SLOTS)
            pe.sem_inc(z_part, 1)

            with pe.Fori(0, BATCH) as b:
                def project0(n, piece):
                    slot = n % XBUF

                    def product(dst, w, x_part, column, first, last_one):
                        for k in range(CT):
                            start = column + k * 2 * D0
                            last = mm(dst, w[:, start:start + 2 * D0], x_part[:, slot, k, :],
                                      start=first and k == 0, stop=last_one and k == CT - 1)
                        return last

                    if piece == QK_HI:
                        pe.wait_ge(p0_xhi, b * NC + (n + 1))
                        if n > LOW_DVE:
                            pe.wait_ge(p0_hi, b * NC + n)
                        elif n >= 2:
                            pe.wait_ge(p0_lo, b * LOW_DVE + n)
                        product(ps[:, qk_bank(n), :], w_hi, xhi, WQK0, True, False)
                        product(ps[:, qk_bank(n), :], w_lo, xhi, WQK0, False, False)
                    elif piece == QK_LO:
                        if n == 0:
                            pe.wait_ge(p0_xlo_first, b + 1)
                        else:
                            pe.wait_ge(p0_xlo, b * (NC - 1) + n)
                        product(ps[:, qk_bank(n), :], w_hi, xlo, WQK0, False, True).then_inc(p0_qk, 1)
                    elif piece == VALUES:
                        if n == 0:
                            pe.wait_ge(p0_lo, b * LOW_DVE + 2)
                        else:
                            pe.wait_ge(p0_vout, b * NC + n)
                        product(ps[:, 1, :], w_hi, xhi, WV0, True, False)
                        product(ps[:, 1, :], w_lo, xhi, WV0, False, False)
                        product(ps[:, 1, :], w_hi, xlo, WV0, False, True).then_inc(p0_v, 1)
                    else:
                        pe.wait_ge(p0_vlo, b * NC + (n + 1))
                        for t in range(TPC):
                            last = mm(ps[:, 1, t * P:(t + 1) * P], vstack[:, n % 2, t * P:(t + 1) * P],
                                      ident_r[:], start=True, stop=True)
                        last.then_inc(p0_turned, 1)

                parts = -1
                for what, *at in ORDER0:
                    if what == "project":
                        project0(*at)
                    elif what == "max":
                        k, t, q = at
                        if max(t // TPW, q) > parts:
                            parts = max(t // TPW, q)
                            complete = CPW * (parts + 1)
                            if complete <= LOW_DVE:
                                pe.wait_ge(p0_lo, b * LOW_DVE + complete)
                            else:
                                pe.wait_ge(p0_lo_pool, b * (NC - LOW_DVE) + (complete - LOW_DVE))
                        if k == 0:
                            pe.wait_ge(y_ready, b * NC + 1)
                        pe.wait_ge(m_free, b * (MTILES + 1) + (k + 1))
                        s = 2 + 2 * (k % MBUF)
                        energy0(ps[:, s:s + 2, :], t, q * WIDE).then_inc(m_energy, 1)

                pe.wait_ge(p0_vout, b * NC + NC)
                pe.wait_ge(m_free, b * (MTILES + 1) + (MTILES + MBUF))

                def energies0(t, h):
                    energy0(ps[:, 2 * (t % EBUF):2 * (t % EBUF) + 2, :], t, h * E0W).then_inc(s0_energy, 1)

                def attend0(t, h):
                    pe.wait_ge(s0_lo, b * STEPS0 + h * NT + (t + 1 + SLOTS))
                    if t == 0:
                        pe.wait_ge(s0_out, b * E0CH + h + 1)
                    for part in (phi, plo):
                        for k in range(E0W // BANK):
                            last = mm(ps[:, 6 + k, :], v0[:, t, :, :].rearrange("p h c -> p (h c)"),
                                      part[:, t % SLOTS, k * BANK:(k + 1) * BANK],
                                      start=t == 0 and part is phi, stop=t == NT - 1 and part is plo)
                    last.then_inc(s0_av, 1)

                def project_out(n):
                    for k in range(CT):
                        last = mm(ps[:, k, :], wo0s[:, k * P:(k + 1) * P], att[:, n * BANK:(n + 1) * BANK],
                                  start=True, stop=True)
                    last.then_inc(wo_done, 1)

                def chunk0(h, final):
                    for t in range(NT):
                        ahead = t + LAG0
                        if ahead < NT or not final:
                            tile = ahead % NT
                            before = ahead - EBUF if ahead < NT else (NT - 1 - (NT - 1 - tile) % EBUF)
                            pe.wait_ge(s0_exp, b * STEPS0 + h * NT + (before + 1))
                            energies0(tile, h + 1 if ahead >= NT else h)
                        if final and t == NT - 1:
                            pe.wait_ge(s0_exp, b * STEPS0 + STEPS0)
                            project_out(0)
                        attend0(t, h)

                for t in range(LAG0):
                    energies0(t, 0)
                with pe.Fori(0, E0CH - 1) as h:
                    chunk0(h, False)
                chunk0(E0CH - 1, True)

                def unit(k, chunk, weights, bank):
                    pe.wait_ge(unit_free, b * (NC * UNITS) + chunk * UNITS + (k + 1))
                    i, j = divmod(k, NC)
                    mm(ps[:, bank + k % 2, :], weights(i), ks[0:K1, j * BANK:(j + 1) * BANK],
                       start=True, stop=True).then_inc(unit_energy, 1)

                def first_unit(i, j):
                    pe.wait_ge(unit_free, b * (NC * UNITS) + (j * TPC + i + 1))
                    mm(ps[:, 2 + i % 2, :], qs[0:K1, i * P:(i + 1) * P], ks[0:K1, j * BANK:(j + 1) * BANK],
                       start=True, stop=True).then_inc(unit_energy, 1)

                pe.wait_ge(x1_ready, b * NC + 1)
                project_out(1)
                parts1 = ((w_hi, xhi), (w_lo, xhi), (w_hi, xlo))
                for n in range(NC):
                    slot = n % XBUF
                    if n + 2 < NC:
                        pe.wait_ge(x1_ready, b * NC + (n + 2))
                        if n + 2 == (E0CH - 1) * E0W // BANK:
                            pe.wait_ge(s0_out, b * E0CH + (E0CH + 1))
                        project_out(n + 2)
                    pe.wait_ge(p1_xlo, b * NC + (n + 1))
                    if n >= 2:
                        pe.wait_ge(p1_lo, b * NC + (n - 1))
                    for w, xp in parts1:
                        for k in range(CT):
                            start = WQK1 + k * 2 * D1
                            last = mm(ps[0:2 * D1, 4 + n % 2, :], w[:, start:start + 2 * D1], xp[:, slot, k, :],
                                      start=w is w_hi and xp is xhi and k == 0,
                                      stop=xp is xlo and k == CT - 1)
                    last.then_inc(p1_qk, 1)
                    if n >= 1:
                        pe.wait_ge(p1_vlo, b * NC + n)
                    for t in range(TPC):
                        for w, xp in parts1:
                            for k in range(CT):
                                last = mm(ps[:, 6 + t // 2, (t % 2) * C:(t % 2 + 1) * C],
                                          xp[:, slot, k, t * P:(t + 1) * P],
                                          w[:, WV1 + k * C:WV1 + (k + 1) * C],
                                          start=w is w_hi and xp is xhi and k == 0,
                                          stop=xp is xlo and k == CT - 1)
                        if t == TPC - 1:
                            last.then_inc(p1_v, 1)
                        if n >= 1:
                            if t == 0:
                                pe.wait_ge(p1_lo, b * NC + n)
                            first_unit(t, n - 1)
                pe.wait_ge(p1_lo, b * NC + NC)
                for i in range(TPC):
                    first_unit(i, NC - 1)

                def turn_rows(n, bank):
                    pe.wait_ge(rows_lo, b * NC + n + 1)
                    for q in range(TPC):
                        last = mm(ps[0:2, bank, q * P:(q + 1) * P], neg_rows[:, q, :], ident_r[:],
                                  start=True, stop=True)
                    last.then_inc(rows_t, 1)

                def energies1(u, n):
                    for j in range(2):
                        t = 2 * u + j
                        last = mm(ps[:, 2 * (u % 2) + j, :], ks[0:K1R, t * P:(t + 1) * P],
                                  qs[0:K1R, cols(n)], start=True, stop=True)
                    last.then_inc(s1_energy, 1)

                def chunk1(n, final):
                    for u in range(PAIRS):
                        if u == ROWS_AT and not final:
                            turn_rows(n + 1, 7)
                        if u + 1 < PAIRS or not final:
                            pe.wait_ge(s1_exp, b * (2 * STEPS1) + n * (2 * PAIRS) + (2 * u + 2))
                            if u + 1 == PAIRS:
                                pe.wait_ge(rows_in, b * NC + n + 2)
                            energies1((u + 1) % PAIRS, n + 1 if u + 1 == PAIRS else n)
                        units = [] if final else list(UNIT_AT.get(u, ()))
                        if units and u == min(UNIT_AT):
                            pe.wait_ge(qnext_set, b * (NC - 1) + n + 1)
                            pe.wait_ge(y_scaled, b * NC + n + 1)
                        pe.wait_ge(s1_exp, b * (2 * STEPS1) + n * (2 * PAIRS) + (2 * u + 2 + 2))
                        if u == 0:
                            pe.wait_ge(s1_out, b * NC + n + 1)
                        for part, lo in ((phi, 0), (phi, 1), (plo, 0)):
                            if part is plo and u == PAIRS - 1:
                                pe.wait_ge(z_sum, b * NC + n + 1)
                                for q in range(TPC):
                                    last = mm(ps[:, 6, q:q + 1], zacc[:, q * P:(q + 1) * P], ones[:],
                                              start=True, stop=True)
                                last.then_inc(z_part, 1)
                            if part is plo:
                                pe.wait_ge(s1_lo, b * STEPS1 + n * PAIRS + (u + 1 + SLOTS))
                            for j in range(2):
                                for k in range(CT):
                                    last = mm(ps[:, 4 + k, :], v1[:, 2 * u + j, lo, k * P:(k + 1) * P],
                                              part[:, u % SLOTS, j * BANK:(j + 1) * BANK],
                                              start=u == 0 and j == 0 and part is phi and lo == 0,
                                              stop=u == PAIRS - 1 and j == 1 and part is plo)
                            if part is plo:
                                last.then_inc(s1_av, 1)
                            if units:
                                unit(units.pop(0), n + 1, lambda i: qnext[:, i * P:(i + 1) * P], 6)
                    pe.wait_ge(z_scale, b * NC + n + 1)
                    for q in range(TPC):
                        last = mm(ps[:, 7, q * P:(q + 1) * P], rzg[:, q:q + 1].to_broadcast([P, P]), ident[:],
                                  start=True, stop=True)
                    last.then_inc(z_rows, 1)

                turn_rows(0, 2)
                pe.wait_ge(rows_in, b * NC + 1)
                pe.wait_ge(ones_set, b + 1)
                energies1(0, 0)
                with pe.Fori(0, NC - 1) as n:
                    chunk1(n, False)
                chunk1(NC - 1, True)

        @block.scalar
        def _(act):
            act.sem_inc(s1_exp, 2)
            act.sem_inc(s0_out, 1)
            act.sem_inc(s1_out, 1)
            act.wait_ge(w_loaded, 16 * 4)
            nc.scalar.copy(w_hi[:], wraw).then_inc(w_rounded, 1)
            nc.scalar.copy(ident_r[:], ident[:]).then_inc(w_rounded, 1)
            with act.Fori(0, BATCH) as b:
                def input0(n):
                    act.wait_ge(x_loaded[n], b * 16 + 16)
                    if n >= XBUF:
                        act.wait_ge(p0_v, b * NC + (n - XBUF + 1))
                    nc.scalar.copy(xhi[:, n % XBUF, :, :], xs[:, :, n * BANK:(n + 1) * BANK]).then_inc(p0_xhi, 1)

                for n in range(XBUF):
                    input0(n)
                for what, *at in ORDER0:
                    if what != "project":
                        continue
                    n, piece = at
                    c = slice(n * BANK, (n + 1) * BANK)
                    s = n % 2
                    if piece == QK_LO:
                        act.wait_ge(p0_qk, b * NC + (n + 1))
                        nc.scalar.activation(qs[0:D0, c], ps[0:D0, qk_bank(n), :], ACT.Identity,
                                             bias=pc[0:D0, BQK0:BQK0 + 1])
                        if n >= LOW_DVE:
                            if n >= LOW_DVE + 2:
                                act.wait_ge(p0_lo_pool, b * (NC - LOW_DVE) + (n - LOW_DVE - 1))
                            nc.scalar.activation(qktmp[:, s, :], ps[:, qk_bank(n), :], ACT.Identity,
                                                 bias=pc[:, BQK0:BQK0 + 1])
                        for half in (0, D0):
                            last = nc.scalar.activation(ks[half:half + D0, c], ps[D0:P, qk_bank(n), :], ACT.Identity,
                                                        bias=pc[D0:P, BQK0:BQK0 + 1])
                        last.then_inc(p0_hi, 1)
                    elif piece == VALUES:
                        act.wait_ge(p0_v, b * NC + (n + 1))
                        if n >= 2:
                            act.wait_ge(p0_vlo, b * NC + (n - 1))
                        for dst in (vtmp, vstack):
                            last = nc.scalar.activation(dst[:, s, :], ps[:, 1, :], ACT.Identity,
                                                        bias=pc[:, BV0:BV0 + 1])
                        last.then_inc(p0_vhi, 1)
                        if n + XBUF < NC:
                            input0(n + XBUF)
                    elif piece == TURN:
                        act.wait_ge(p0_turned, b * NC + (n + 1))
                        nc.scalar.copy(vs[:, c], ps[:, 1, :]).then_inc(p0_vout, 1)
                act.wait_ge(p0_v, b * NC + NC)
                act.wait_ge(p0_xlo, b * (NC - 1) + (NC - 1))
                act.wait_ge(consts_set, 3)
                for k in range(CT):
                    nc.scalar.activation(xs[:, k, :], xs[:, k, :], ACT.Identity,
                                         bias=gbo[:, k:k + 1]).then_inc(x_biased, 1)
                act.wait_ge(gmax_full, b + 1)
                nc.scalar.mul(neg_max[:], gmax_all[:], -1.0).then_inc(neg_set, 1)
                act.wait_ge(neg_set, b + 1)

                def exp0(t, h):
                    act.wait_ge(s0_energy, b * STEPS0 + h * NT + (t + 1))
                    act.wait_ge(s0_lo, b * STEPS0 + h * NT + (t + 1))
                    s = 2 * (t % NT % EBUF)
                    nc.scalar.activation(prob[:, t % SLOTS, :].rearrange("p (k n) -> p k n", k=2),
                                         ps[:, s:s + 2, :], ACT.Exp, bias=neg_max[:],
                                         accum_out=sums[:, bass.ds(h * NT + t, 1)]).then_inc(s0_exp, 1)

                def move_out0(h):
                    act.wait_ge(s0_av, b * STEPS0 + h * NT + (NT + SLOTS))
                    nc.scalar.copy(att[:, bass.ds(h * E0W, E0W)].rearrange("p (k n) -> p k n", k=2),
                                   ps[:, 6:8, :]).then_inc(s0_out, 1)

                for t in range(LAG0):
                    exp0(t, 0)
                with act.Fori(0, E0CH - 1) as h:
                    for t in range(LAG0, NT + LAG0):
                        exp0(t, h)
                    move_out0(h)
                for t in range(LAG0, NT):
                    exp0(t, E0CH - 1)
                move_out0(E0CH - 1)

                def input1(n):
                    act.wait_ge(x1_ready, b * NC + (n + 1))
                    if n >= XBUF:
                        act.wait_ge(p1_v, b * NC + (n - XBUF + 1))
                    nc.scalar.copy(xhi[:, n % XBUF, :, :], xs[:, :, n * BANK:(n + 1) * BANK]).then_inc(p1_xhi, 1)

                input1(0)
                input1(1)
                for n in range(NC):
                    c = slice(n * BANK, (n + 1) * BANK)
                    act.wait_ge(p1_qk, b * NC + (n + 1))
                    for dst, rows, src in ((qs, 0, 0), (qs, 2, 0), (ks, 0, 1), (ks, 1, 1)):
                        last = nc.scalar.activation(dst[rows * D1:(rows + 1) * D1, c],
                                                    ps[src * D1:(src + 1) * D1, 4 + n % 2, :], ACT.Identity,
                                                    bias=pc[src * D1:(src + 1) * D1, BQK1:BQK1 + 1])
                    last.then_inc(p1_hi, 1)
                    if n + 2 < NC:
                        input1(n + 2)
                    act.wait_ge(p1_v, b * NC + (n + 1))
                    nc.scalar.copy(v1[:, n * TPC:(n + 1) * TPC, 0, :],
                                   ps[:, 6:8, :].rearrange("p k (t c) -> p (k t) c", c=C)).then_inc(p1_vhi, 1)

                def insert_rows(n, bank):
                    act.wait_ge(rows_t, b * NC + n + 1)
                    nc.scalar.copy(qs[K1:K1R, cols(n)], ps[0:2, bank, :]).then_inc(rows_in, 1)

                def exp1(u, n):
                    act.wait_ge(s1_energy, b * STEPS1 + n * PAIRS + (u + 1))
                    act.wait_ge(s1_lo, b * STEPS1 + n * PAIRS + (u + 1))
                    act.wait_ge(s1_sum, b * STEPS1 + n * PAIRS + (u + 1))
                    s = 2 * (u % 2)
                    nc.scalar.activation(prob[:, u % SLOTS, :].rearrange("p (k n) -> p k n", k=2),
                                         ps[:, s:s + 2, :], ACT.Exp).then_inc(s1_exp, 1)
                    act.wait_ge(s1_av, b * STEPS1 + n * PAIRS + (u + 1))
                    nc.scalar.activation(phi[:, u % SLOTS, :].rearrange("p (k n) -> p k n", k=2),
                                         ps[:, s:s + 2, :], ACT.Exp).then_inc(s1_exp, 1)

                def chunk1(n, final):
                    for u in range(PAIRS):
                        if u + 1 < PAIRS or not final:
                            exp1(u + 1, n)
                        if u == ROWS_AT and not final:
                            insert_rows(n + 1, 7)
                    act.wait_ge(s1_av, b * STEPS1 + n * PAIRS + (PAIRS + SLOTS))
                    nc.scalar.copy(raw, ps[:, 4:6, :]).then_inc(s1_out, 1)

                insert_rows(0, 2)
                exp1(0, 0)
                with act.Fori(0, NC - 1) as n:
                    chunk1(n, False)
                chunk1(NC - 1, True)

        @block.gpsimd
        def _(pool):
            pool.sem_inc(s1_sum, SLOTS)
            with pool.Fori(0, BATCH) as b:
                def input0(n):
                    pool.wait_ge(p0_xhi, b * NC + (n + 1))
                    nc.gpsimd.tensor_tensor(xlo[:, n % XBUF, :, :], xs[:, :, n * BANK:(n + 1) * BANK],
                                            xhi[:, n % XBUF, :, :].bitcast(F32),
                                            ALU.subtract).then_inc(p0_xlo, 1)

                for n in range(1, XBUF):
                    input0(n)
                inputs = XBUF
                for what, *at in ORDER0:
                    if what == "project" and at[1] == VALUES:
                        n = at[0]
                        pool.wait_ge(p0_vhi, b * NC + (n + 1))
                        pool.wait_ge(p0_xlo, b * (NC - 1) + (inputs - 1))
                        nc.gpsimd.tensor_tensor(vstack[D0:P, n % 2, :], vtmp[D0:P, n % 2, :],
                                                vstack[D0:P, n % 2, :].bitcast(F32),
                                                ALU.subtract).then_inc(p0_vlo, 1)
                        pool.wait_ge(p0_vlo, b * NC + (n + 1))
                        if inputs < NC:
                            input0(inputs)
                            inputs += 1
                    elif what == "low" and at[0] >= LOW_DVE:
                        n = at[0]
                        c = slice(n * BANK, (n + 1) * BANK)
                        pool.wait_ge(p0_hi, b * NC + (n + 1))
                        pool.wait_ge(p0_xlo, b * (NC - 1) + (inputs - 1))
                        nc.gpsimd.tensor_tensor(qs[D0:P, c], qktmp[0:D0, n % 2, :], qs[0:D0, c].bitcast(F32),
                                                ALU.subtract).then_inc(p0_qlo, 1)
                        pool.wait_ge(p0_qlo, b * (NC - LOW_DVE) + (n - LOW_DVE + 1))
                        nc.gpsimd.tensor_tensor(k0lo[:, c], qktmp[D0:P, n % 2, :], ks[D0:P, c].bitcast(F32),
                                                ALU.subtract).then_inc(p0_lo_pool, 1)
                        pool.wait_ge(p0_lo_pool, b * (NC - LOW_DVE) + (n - LOW_DVE + 1))
                pool.wait_ge(m_free, b * (MTILES + 1) + (MTILES + MBUF + 1))
                settled(pool)
                nc.gpsimd.partition_all_reduce(gmax_all[:], gmax[:], P,
                                               bass.bass_isa.ReduceOp.max).then_inc(gmax_full, 1)
                with pool.Fori(0, E0CH) as h:
                    for t in range(NT):
                        pool.wait_ge(s0_exp, b * STEPS0 + h * NT + (t + 1))
                        pool.wait_ge(s0_av, b * STEPS0 + h * NT + (t + 1))
                        settled(pool)
                        nc.gpsimd.tensor_scalar(phi[:, t % SLOTS, :], prob[:, t % SLOTS, :], 1.0, 0.0,
                                                ALU.mult, ALU.add).then_inc(s0_hi, 1)
                pool.wait_ge(sum_part, b + 1)
                settled(pool)
                nc.gpsimd.partition_all_reduce(psum0_all[:], psum0[:], P,
                                               bass.bass_isa.ReduceOp.add).then_inc(sum_full, 1)
                pool.wait_ge(sum_full, b + 1)
                for n in range(NC):
                    pool.wait_ge(p1_xhi, b * NC + (n + 1))
                    nc.gpsimd.tensor_tensor(xlo[:, n % XBUF, :, :], xs[:, :, n * BANK:(n + 1) * BANK],
                                            xhi[:, n % XBUF, :, :].bitcast(F32),
                                            ALU.subtract).then_inc(p1_xlo, 1)
                pool.wait_ge(p1_xlo, b * NC + NC)
                settled(pool)
                nc.gpsimd.memset(ks[K1:K1R, :].bitcast(F32), 1.0).then_inc(ones_set, 1)
                pool.wait_ge(ones_set, b + 1)
                settled(pool)
                with pool.Fori(0, NC) as n:
                    pool.wait_ge(z_part, b * NC + (n + 1))
                    for u in range(PAIRS):
                        pool.wait_ge(s1_exp, b * (2 * STEPS1) + n * (2 * PAIRS) + (2 * u + 1 + 2))
                        if u == 0:
                            settled(pool)
                            nc.gpsimd.tensor_scalar(zacc, prob[:, 0, :], 1.0, 0.0,
                                                    ALU.mult, ALU.add).then_inc(s1_sum, 1)
                            continue
                        pool.wait_ge(s1_sum, b * STEPS1 + n * PAIRS + (u + SLOTS))
                        nc.gpsimd.tensor_tensor(zacc, zacc, prob[:, u % SLOTS, :],
                                                ALU.add).then_inc(s1_sum, 1)

        @block.vector
        def _(dve):
            nc.vector.memset(ones[:], 1.0).then_inc(consts_set, 1)
            dve.sem_inc(m_free, MBUF)
            dve.sem_inc(s0_lo, SLOTS)
            dve.sem_inc(s1_lo, SLOTS)
            dve.sem_inc(unit_free, 2)
            dve.sem_inc(y_scaled, 1)
            dve.sem_inc(y_ready, 1)
            dve.wait_ge(w_loaded, 16 * 4)
            nc.vector.tensor_scalar(gbo[:], pc[:, BO0:BO0 + CT], pc[:, G0:G0 + 1], None,
                                    ALU.mult).then_inc(consts_set, 1)
            nc.vector.tensor_scalar(gbv[:], pc[:, BV1:BV1 + CT], pc[:, G1:G1 + 1], None,
                                    ALU.mult).then_inc(consts_set, 1)
            dve.wait_ge(w_rounded, 1)
            nc.vector.tensor_tensor(w_lo[:], wraw, w_hi[:].bitcast(F32), ALU.subtract).then_inc(w_split, 1)
            with dve.Fori(0, BATCH) as b:
                def low(out, src, bias, hi):
                    return nc.vector.scalar_tensor_tensor(out=out, in0=src, scalar=bias, in1=hi.bitcast(F32),
                                                          op0=ALU.add, op1=ALU.subtract)

                dve.wait_ge(p0_xhi, b * NC + 1)
                nc.vector.tensor_tensor(xlo[:, 0, :, :], xs[:, :, 0:BANK], xhi[:, 0, :, :].bitcast(F32),
                                        ALU.subtract).then_inc(p0_xlo_first, 1)
                for what, *at in ORDER0:
                    if what == "low" and at[0] < LOW_DVE:
                        [n] = at
                        c = slice(n * BANK, (n + 1) * BANK)
                        dve.wait_ge(p0_hi, b * NC + (n + 1))
                        low(qs[D0:P, c], ps[0:D0, qk_bank(n), :], pc[0:D0, BQK0:BQK0 + 1], qs[0:D0, c])
                        low(k0lo[:, c], ps[D0:P, qk_bank(n), :], pc[D0:P, BQK0:BQK0 + 1],
                            ks[D0:P, c]).then_inc(p0_lo, 1)
                    elif what == "max":
                        k = at[0]
                        dve.wait_ge(m_energy, b * MTILES + (k + 1))
                        s = 2 + 2 * (k % MBUF)
                        nc.vector.tensor_reduce(rmax[:, k:k + 1], ps[:, s:s + 2, :], AX.XY,
                                                ALU.max).then_inc(m_free, 1)
                dve.wait_ge(m_free, b * (MTILES + 1) + (MTILES + MBUF))
                nc.vector.tensor_reduce(gmax[:], rmax[:], AX.X, ALU.max).then_inc(m_free, 1)

                with dve.Fori(0, E0CH) as h:
                    for t in range(NT):
                        dve.wait_ge(s0_hi, b * STEPS0 + h * NT + (t + 1))
                        nc.vector.tensor_tensor(plo[:, t % SLOTS, :], prob[:, t % SLOTS, :],
                                                phi[:, t % SLOTS, :].bitcast(F32),
                                                ALU.subtract).then_inc(s0_lo, 1)
                dve.wait_ge(s0_exp, b * STEPS0 + STEPS0)
                nc.vector.tensor_reduce(psum0[:], sums[:], AX.X, ALU.add).then_inc(sum_part, 1)
                dve.wait_ge(sum_full, b + 1)
                nc.vector.reciprocal(rsum0[:], psum0_all[:]).then_inc(rsum_set, 1)
                dve.wait_ge(rsum_set, b + 1)
                nc.vector.tensor_scalar(gscale0[:], rsum0[:], pc[:, G0:G0 + 1], None,
                                        ALU.mult).then_inc(scale_set, 1)
                dve.wait_ge(scale_set, b + 1)
                dve.wait_ge(x_biased, b * CT + CT)

                def input1(n):
                    c = slice(n * BANK, (n + 1) * BANK)
                    dve.wait_ge(wo_done, b * NC + (n + 1))
                    nc.vector.scalar_tensor_tensor(out=xs[:, :, c], in0=ps[:, 0:2, :], scalar=gscale0[:],
                                                   in1=xs[:, :, c], op0=ALU.mult, op1=ALU.add).then_inc(x1_ready, 1)

                def reduce_unit(k, chunk, i, j, bank):
                    dve.wait_ge(unit_energy, b * (NC * UNITS) + chunk * UNITS + (k + 1))
                    nc.vector.tensor_reduce(unit_max[:, i, j:j + 1], ps[:, bank + k % 2, :], AX.X,
                                            ALU.max).then_inc(unit_free, 1)

                def low_values1(n):
                    dve.wait_ge(p1_vhi, b * NC + (n + 1))
                    nc.vector.tensor_tensor(v1[:, n * TPC:(n + 1) * TPC, 1, :],
                                            ps[:, 6:8, :].rearrange("p k (t c) -> p (k t) c", c=C),
                                            v1[:, n * TPC:(n + 1) * TPC, 0, :].bitcast(F32),
                                            ALU.subtract).then_inc(p1_vlo, 1)

                def first_units(j, begin, end):
                    for i in range(begin, end):
                        reduce_unit(j * TPC + i, 0, i, j, 2)

                input1(0)
                input1(1)
                for n in range(NC):
                    c = slice(n * BANK, (n + 1) * BANK)
                    if n + 2 < NC:
                        input1(n + 2)
                    if n >= 1:
                        first_units(n - 1, 0, TPC // 2)
                    dve.wait_ge(p1_hi, b * NC + (n + 1))
                    low(qs[D1:2 * D1, c], ps[0:D1, 4 + n % 2, :], pc[0:D1, BQK1:BQK1 + 1], qs[0:D1, c])
                    low(ks[2 * D1:K1, c], ps[D1:2 * D1, 4 + n % 2, :], pc[D1:2 * D1, BQK1:BQK1 + 1],
                        ks[D1:2 * D1, c]).then_inc(p1_lo, 1)
                    if n >= 1:
                        first_units(n - 1, TPC // 2, TPC)
                    if n + 1 < NC:
                        low_values1(n)
                first_units(NC - 1, 0, TPC)

                def split_rows(n):
                    dve.wait_ge(unit_free, b * (NC * UNITS) + n * UNITS + (UNITS + 2))
                    nc.vector.tensor_reduce(row_max[:], unit_max[:], AX.X, ALU.max).then_inc(rows_max, 1)
                    dve.wait_ge(rows_max, b * NC + n + 1)
                    nc.vector.tensor_scalar(neg_rows[:, :, 0], row_max[:], -1.0, None,
                                            ALU.mult).then_inc(rows_hi, 1)
                    dve.wait_ge(rows_hi, b * NC + n + 1)
                    nc.vector.scalar_tensor_tensor(out=neg_rows[:, :, 1], in0=row_max[:], scalar=-1.0,
                                                   in1=neg_rows[:, :, 0].bitcast(F32), op0=ALU.mult,
                                                   op1=ALU.subtract).then_inc(rows_lo, 1)

                def low1(u, n):
                    dve.wait_ge(s1_exp, b * (2 * STEPS1) + n * (2 * PAIRS) + (2 * u + 2 + 2))
                    nc.vector.tensor_tensor(plo[:, u % SLOTS, :], prob[:, u % SLOTS, :],
                                            phi[:, u % SLOTS, :].bitcast(F32),
                                            ALU.subtract).then_inc(s1_lo, 1)

                def chunk1(n, final):
                    if not final:
                        nc.vector.tensor_copy(qnext[:], qs[0:K1, cols(n + 1)]).then_inc(qnext_set, 1)
                    for u in range(PAIRS):
                        if u == PAIRS - 1:
                            dve.wait_ge(s1_sum, b * STEPS1 + n * PAIRS + (PAIRS + SLOTS))
                            nc.vector.tensor_tensor(zacc[:, 0:BANK], zacc[:, 0:BANK], zacc[:, BANK:2 * BANK],
                                                    ALU.add).then_inc(z_sum, 1)
                            if not final:
                                low1(PAIRS, n)
                            dve.wait_ge(z_part, b * NC + n + 2)
                            nc.vector.reciprocal(rz[:], ps[:, 6, 0:TPC]).then_inc(z_recip, 1)
                            dve.wait_ge(z_recip, b * NC + n + 1)
                            nc.vector.tensor_scalar(rzg[:], rz[:], pc[:, G1:G1 + 1], None,
                                                    ALU.mult).then_inc(z_scale, 1)
                        units = [] if final else list(UNIT_AT.get(u, ()))
                        for k in units[:2]:
                            reduce_unit(k, n + 1, *divmod(k, NC), 6)
                        if u + 1 < PAIRS:
                            low1(u + 1, n)
                        for k in units[2:]:
                            reduce_unit(k, n + 1, *divmod(k, NC), 6)
                        if units and u == max(UNIT_AT):
                            split_rows(n + 1)
                    dve.wait_ge(z_rows, b * NC + n + 1)
                    dve.wait_ge(s1_out, b * NC + n + 2)
                    for k in range(CT):
                        last = nc.vector.tensor_tensor(raw[:, k, :], ps[:, 7, :], raw[:, k, :], ALU.mult)
                    last.then_inc(y_scaled, 1)
                    dve.wait_ge(y_scaled, b * NC + n + 2)
                    for k in range(CT):
                        last = nc.vector.scalar_tensor_tensor(out=xs[:, k, cols(n)], in0=raw[:, k, :],
                                                              scalar=gbv[:, k:k + 1], in1=xs[:, k, cols(n)],
                                                              op0=ALU.add, op1=ALU.add)
                    last.then_inc(y_ready, 1)

                split_rows(0)
                low_values1(NC - 1)
                low1(0, 0)
                with dve.Fori(0, NC - 1) as n:
                    chunk1(n, False)
                chunk1(NC - 1, True)


def kernel(x, L0_conv_Wq, L0_conv_bq, L0_conv_Wk, L0_conv_bk, L0_conv_Wv, L0_conv_bv, L0_conv_Wo,
           L0_conv_bo, L0_conv_gamma, L1_conv_Wq, L1_conv_bq, L1_conv_Wk, L1_conv_bk, L1_conv_Wv,
           L1_conv_bv, L1_conv_gamma):
    import numpy as np
    import concourse.bacc as bacc
    from concourse import mybir as mb
    from concourse.bass_utils import run_bass_kernel_spmd

    def channels(w):
        return np.ascontiguousarray(np.asarray(w).T.reshape(CT, P, -1).transpose(1, 0, 2))

    f = np.float32
    a = {n: np.asarray(v) for n, v in locals().items() if n.startswith("L") or n == "x"}
    wq0, wk0 = a["L0_conv_Wq"], a["L0_conv_Wk"]
    wq1, wk1 = a["L1_conv_Wq"], a["L1_conv_Wk"]
    percol = np.zeros((P, NPC), f)
    percol[:, BQK0] = np.concatenate([a["L0_conv_bq"], a["L0_conv_bk"]])
    percol[0:2 * D1, BQK1] = np.concatenate([a["L1_conv_bq"], a["L1_conv_bk"]])
    percol[:, BO0:BO0 + CT] = a["L0_conv_bo"].reshape(CT, P).T
    percol[:, BV1:BV1 + CT] = a["L1_conv_bv"].reshape(CT, P).T
    percol[:, BV0] = np.concatenate([a["L0_conv_bv"]] * 2)
    percol[:, G0] = a["L0_conv_gamma"][0]
    percol[:, G1] = a["L1_conv_gamma"][0]
    arrays = {
        "x_in": np.ascontiguousarray(a["x"].reshape(BATCH, CT, P, N).transpose(0, 2, 1, 3)),
        "w_parts": np.concatenate([channels(np.concatenate([wq0, wk0])).reshape(P, -1),
                                   channels(np.concatenate([a["L0_conv_Wv"]] * 2)).reshape(P, -1),
                                   channels(np.concatenate([wq1, wk1])).reshape(P, -1),
                                   channels(a["L1_conv_Wv"]).reshape(P, -1)], axis=1),
        "w_o0": np.ascontiguousarray(np.concatenate([a["L0_conv_Wo"].T] * 2)),
        "per_col": percol,
        "identity": np.eye(P, dtype=f),
    }
    nc = bacc.Bacc("TRN2", target_bir_lowering=False, num_devices=1)
    args = [nc.dram_tensor(n, v.shape, mb.dt.from_np(v.dtype), kind="ExternalInput").ap()
            for n, v in arrays.items()]
    y = nc.dram_tensor("y_out", (BATCH, P, CT, N), mb.dt.float32, kind="ExternalOutput").ap()
    build(nc, *args, y)
    r = run_bass_kernel_spmd(nc, [arrays], core_ids=[0])
    got = np.asarray(r.results[0]["y_out"])
    return np.ascontiguousarray(got.transpose(0, 2, 1, 3)).reshape(BATCH, C, 64, 64)
```
